# Optimizing a Trainium2 kernel written in Bass

```python
import numpy as np
import jax
import jax.numpy as jnp

def _softmax(x, axis=-1):
    return jax.nn.softmax(x, axis=axis)

def _gelu(x):
    return jax.nn.gelu(x, approximate=True)

def _silu(x):
    return jax.nn.silu(x)

def _sigmoid(x):
    return jax.nn.sigmoid(x)

def _layernorm(x, axis=-1, eps=1e-05):
    m = jnp.mean(x, axis=axis, keepdims=True)
    v = jnp.var(x, axis=axis, keepdims=True)
    return (x - m) / jnp.sqrt(v + eps)

def _scatter_add(tgt, idx, src, axis=0):
    return tgt.at[idx].add(src)

def _segment_sum(src, seg, n):
    return jax.ops.segment_sum(src, seg, n)
kernel_name = 'mk_sandwich_d1_jaxref_r8_e3bcec'

def setup_inputs(seed: int=0):
    np.random.seed(seed)
    _w = jnp.asarray

    def _L0_attn_setup():
        import jax, jax.numpy as jnp
        import numpy as np
        B, L, D_MODEL, D_INNER, D_STATE, DT_RANK, K = (2, 128, 128, 256, 16, 64, 4)
        key = jax.random.key(seed)
        ks = jax.random.split(key, 8)
        sc = lambda n: 1.0 / np.sqrt(n)
        return {'x': jax.random.normal(ks[0], (B, L, D_MODEL), jnp.float32), 'W_in': jax.random.normal(ks[1], (2 * D_INNER, D_MODEL), jnp.float32) * sc(D_MODEL), 'conv_w': jax.random.normal(ks[2], (D_INNER, K), jnp.float32) * sc(K), 'conv_b': jax.random.normal(ks[3], (D_INNER,), jnp.float32) * 0.1, 'W_x': jax.random.normal(ks[4], (DT_RANK + 2 * D_STATE, D_INNER), jnp.float32) * sc(D_INNER), 'W_dt': jax.random.normal(ks[5], (D_INNER, DT_RANK), jnp.float32) * sc(DT_RANK), 'b_dt': jax.random.normal(ks[6], (D_INNER,), jnp.float32) * 0.1, 'A_log': jnp.log(jnp.tile(jnp.arange(1.0, D_STATE + 1.0, dtype=jnp.float32)[None, :], (D_INNER, 1))), 'Dp': jnp.ones((D_INNER,), jnp.float32), 'W_out': jax.random.normal(ks[7], (D_MODEL, D_INNER), jnp.float32) * sc(D_INNER)}
    _L0_attn_in = _L0_attn_setup()

    def _L0_ffn_setup():
        import jax, jax.numpy as jnp
        import numpy as np
        D = 128
        H = 4
        DF = 512
        E = 8
        EPS = 1e-05

        def _layer_norm(x, g, b):
            mu = jnp.mean(x, axis=-1, keepdims=True)
            var = jnp.mean(jnp.square(x - mu), axis=-1, keepdims=True)
            return (x - mu) * jax.lax.rsqrt(var + EPS) * g + b

        def _mha(x, Wqkv, bqkv, Wo, bo):
            S, B, _ = x.shape
            hd = D // H
            qkv = x @ Wqkv.T + bqkv
            q, k, v = jnp.split(qkv, 3, axis=-1)
            to_heads = lambda t: t.reshape(S, B, H, hd).transpose(1, 2, 0, 3)
            q, k, v = (to_heads(q), to_heads(k), to_heads(v))
            scores = jnp.einsum('bhqd,bhkd->bhqk', q, k) * (1.0 / np.sqrt(hd))
            att = jax.nn.softmax(scores, axis=-1)
            o = jnp.einsum('bhqk,bhkd->bhqd', att, v)
            o = o.transpose(2, 0, 1, 3).reshape(S, B, D)
            return o @ Wo.T + bo

        def _moe(x, Wg, W1, b1, W2, b2):
            S, B, _ = x.shape
            xf = x.reshape(S * B, D)
            logits = xf @ Wg.T
            idx = jnp.argmax(logits, axis=-1)
            out = jnp.zeros_like(xf)
            for e in range(E):
                m = (idx == e)[:, None].astype(xf.dtype)
                h = jax.nn.relu(xf @ W1[e] + b1[e])
                out = out + m * (h @ W2[e] + b2[e])
            return out.reshape(S, B, D)
        key = jax.random.key(seed)
        ks = jax.random.split(key, 16)
        S, B = (64, 8)
        s = lambda k, shape, fan: jax.random.normal(k, shape, jnp.float32) * (1.0 / np.sqrt(fan))
        return {'x': jax.random.normal(ks[0], (S, B, D), jnp.float32), 'Wqkv': s(ks[1], (3 * D, D), D), 'bqkv': jnp.zeros((3 * D,), jnp.float32), 'Wo': s(ks[2], (D, D), D), 'bo': jnp.zeros((D,), jnp.float32), 'g1': jnp.ones((D,), jnp.float32), 'be1': jnp.zeros((D,), jnp.float32), 'g2': jnp.ones((D,), jnp.float32), 'be2': jnp.zeros((D,), jnp.float32), 'Wg': s(ks[3], (E, D), D), 'W1': s(ks[4], (E, D, DF), D), 'b1': jnp.zeros((E, DF), jnp.float32), 'W2': s(ks[5], (E, DF, D), DF), 'b2': jnp.zeros((E, D), jnp.float32)}
    _L0_ffn_in = _L0_ffn_setup()
    _d = {'L0_attn_x': _L0_attn_in['x'], 'L0_attn_W_in': _L0_attn_in['W_in'], 'L0_attn_conv_w': _L0_attn_in['conv_w'], 'L0_attn_conv_b': _L0_attn_in['conv_b'], 'L0_attn_W_x': _L0_attn_in['W_x'], 'L0_attn_W_dt': _L0_attn_in['W_dt'], 'L0_attn_b_dt': _L0_attn_in['b_dt'], 'L0_attn_A_log': _L0_attn_in['A_log'], 'L0_attn_Dp': _L0_attn_in['Dp'], 'L0_attn_W_out': _L0_attn_in['W_out'], 'L0_ffn_Wqkv': _L0_ffn_in['Wqkv'], 'L0_ffn_bqkv': _L0_ffn_in['bqkv'], 'L0_ffn_Wo': _L0_ffn_in['Wo'], 'L0_ffn_bo': _L0_ffn_in['bo'], 'L0_ffn_g1': _L0_ffn_in['g1'], 'L0_ffn_be1': _L0_ffn_in['be1'], 'L0_ffn_g2': _L0_ffn_in['g2'], 'L0_ffn_be2': _L0_ffn_in['be2'], 'L0_ffn_Wg': _L0_ffn_in['Wg'], 'L0_ffn_W1': _L0_ffn_in['W1'], 'L0_ffn_b1': _L0_ffn_in['b1'], 'L0_ffn_W2': _L0_ffn_in['W2'], 'L0_ffn_b2': _L0_ffn_in['b2']}
    _x0 = _d['L0_attn_x']
    _d['L0_attn_x'] = jax.random.normal(jax.random.fold_in(jax.random.key(seed), 1), (8, 1024, 128), dtype=_x0.dtype)
    del _x0
    return _d

def reference(L0_attn_x, L0_attn_W_in, L0_attn_conv_w, L0_attn_conv_b, L0_attn_W_x, L0_attn_W_dt, L0_attn_b_dt, L0_attn_A_log, L0_attn_Dp, L0_attn_W_out, L0_ffn_Wqkv, L0_ffn_bqkv, L0_ffn_Wo, L0_ffn_bo, L0_ffn_g1, L0_ffn_be1, L0_ffn_g2, L0_ffn_be2, L0_ffn_Wg, L0_ffn_W1, L0_ffn_b1, L0_ffn_W2, L0_ffn_b2):

    def _L0_attn_ref(x, W_in, conv_w, conv_b, W_x, W_dt, b_dt, A_log, Dp, W_out):
        import jax, jax.numpy as jnp
        import numpy as np
        B, L, D_MODEL, D_INNER, D_STATE, DT_RANK, K = (2, 128, 128, 256, 16, 64, 4)
        xz = x @ W_in.T
        xc, z = jnp.split(xz, 2, axis=-1)
        d_inner = xc.shape[-1]
        k = conv_w.shape[1]
        xt = xc.transpose(0, 2, 1)
        yt = jax.lax.conv_general_dilated(xt, conv_w[:, None, :], window_strides=(1,), padding=[(k - 1, 0)], dimension_numbers=('NCH', 'OIH', 'NCH'), feature_group_count=d_inner)
        xc = yt.transpose(0, 2, 1) + conv_b
        xc = jax.nn.silu(xc)
        dBC = xc @ W_x.T
        dt_rank = W_dt.shape[1]
        d_state = A_log.shape[1]
        delta = dBC[..., :dt_rank]
        Bm = dBC[..., dt_rank:dt_rank + d_state]
        Cm = dBC[..., dt_rank + d_state:]
        delta = jax.nn.softplus(delta @ W_dt.T + b_dt)
        A = -jnp.exp(A_log)
        deltaA = jnp.exp(delta[..., None] * A)
        BX = delta[..., None] * Bm[:, :, None, :] * xc[..., None]

        def combine(e1, e2):
            a1, x1 = e1
            a2, x2 = e2
            return (a1 * a2, a2 * x1 + x2)
        _, hs = jax.lax.associative_scan(combine, (deltaA, BX), axis=1)
        y = jnp.einsum('bldn,bln->bld', hs, Cm) + Dp * xc
        out = y * jax.nn.silu(z) @ W_out.T
        return out

    def _L0_ffn_ref(x, Wqkv, bqkv, Wo, bo, g1, be1, g2, be2, Wg, W1, b1, W2, b2):
        import jax, jax.numpy as jnp
        import numpy as np
        D = 128
        H = 4
        DF = 512
        E = 8
        EPS = 1e-05

        def _layer_norm(x, g, b):
            mu = jnp.mean(x, axis=-1, keepdims=True)
            var = jnp.mean(jnp.square(x - mu), axis=-1, keepdims=True)
            return (x - mu) * jax.lax.rsqrt(var + EPS) * g + b

        def _mha(x, Wqkv, bqkv, Wo, bo):
            S, B, _ = x.shape
            hd = D // H
            qkv = x @ Wqkv.T + bqkv
            q, k, v = jnp.split(qkv, 3, axis=-1)
            to_heads = lambda t: t.reshape(S, B, H, hd).transpose(1, 2, 0, 3)
            q, k, v = (to_heads(q), to_heads(k), to_heads(v))
            scores = jnp.einsum('bhqd,bhkd->bhqk', q, k) * (1.0 / np.sqrt(hd))
            att = jax.nn.softmax(scores, axis=-1)
            o = jnp.einsum('bhqk,bhkd->bhqd', att, v)
            o = o.transpose(2, 0, 1, 3).reshape(S, B, D)
            return o @ Wo.T + bo

        def _moe(x, Wg, W1, b1, W2, b2):
            S, B, _ = x.shape
            xf = x.reshape(S * B, D)
            logits = xf @ Wg.T
            idx = jnp.argmax(logits, axis=-1)
            out = jnp.zeros_like(xf)
            for e in range(E):
                m = (idx == e)[:, None].astype(xf.dtype)
                h = jax.nn.relu(xf @ W1[e] + b1[e])
                out = out + m * (h @ W2[e] + b2[e])
            return out.reshape(S, B, D)
        y = _layer_norm(x + _mha(x, Wqkv, bqkv, Wo, bo), g1, be1)
        z = _layer_norm(y + _moe(y, Wg, W1, b1, W2, b2), g2, be2)
        return z
    x = L0_attn_x
    x = x + _layernorm(_L0_attn_ref(_layernorm(x, axis=-1), L0_attn_W_in, L0_attn_conv_w, L0_attn_conv_b, L0_attn_W_x, L0_attn_W_dt, L0_attn_b_dt, L0_attn_A_log, L0_attn_Dp, L0_attn_W_out), axis=-1)
    x = x + _layernorm(_L0_ffn_ref(_layernorm(x, axis=-1), L0_ffn_Wqkv, L0_ffn_bqkv, L0_ffn_Wo, L0_ffn_bo, L0_ffn_g1, L0_ffn_be1, L0_ffn_g2, L0_ffn_be2, L0_ffn_Wg, L0_ffn_W1, L0_ffn_b1, L0_ffn_W2, L0_ffn_b2), axis=-1)
    return x

_drawn_inputs = setup_inputs


def setup_inputs(seed=0):
    import zlib

    import numpy as np

    out = dict(_drawn_inputs(seed))
    spreads = {'L0_attn_Dp': (1.0, 0.2),
     'L0_ffn_bqkv': (0.0, 0.1),
     'L0_ffn_bo': (0.0, 0.1),
     'L0_ffn_g1': (1.0, 0.2),
     'L0_ffn_be1': (0.0, 0.1),
     'L0_ffn_g2': (1.0, 0.2),
     'L0_ffn_be2': (0.0, 0.1),
     'L0_ffn_b1': (0.0, 0.333),
     'L0_ffn_b2': (0.0, 0.1)}
    factors = {}
    for name, (base, spread) in spreads.items():
        noise = np.random.default_rng([zlib.crc32(name.encode()), seed]).standard_normal(out[name].shape)
        drawn = base * np.exp(spread * noise) if base else spread * noise
        out[name] = jnp.asarray(drawn.astype(out[name].dtype))
    for name, factor in factors.items():
        out[name] = (out[name] * factor).astype(out[name].dtype)
    return out
```

```python
from contextlib import ExitStack

import concourse.bass as bass
from concourse import mybir

ALU = mybir.AluOpType
ACT = mybir.ActivationFunctionType
AX = mybir.AxisListType
F32 = mybir.dt.float32
BF16 = mybir.dt.bfloat16
I32 = mybir.dt.int32
P = 128

SEQS, LENGTH, D = 8, 1024, 128
DI, NST, RANK, TAPS = 256, 16, 64, 4
HEADS, HD, EXPERTS, DF = 4, 32, 8, 512
EPS = 1e-5
HALF = 512
STEPS = SEQS * LENGTH // HALF
CH = DI // P
TT = HALF // P
RING = 4
TAIL_SKIP = 3
TAIL_OUT = 12
LN_SET = "natural_log_exp_and_others"


def mamba(nc, sem, carrier, banks, sel, ident, half_neg, x, w_in_t, per_channel, w_x_t, w_dt_t, w_out_t, x1, late_loads, s_late):
    ctx = ExitStack()

    def sb(name, shape, dt=F32):
        return ctx.enter_context(nc.sbuf_tensor(name, shape, dt))

    with ctx:
        ps_y, ps_b, ps_c = banks[0:2], banks[2:4], banks[4:6]
        m0, m1 = banks[6:8]

        w_in = sb("w_in", [P, 2 * DI])
        chan = sb("chan", [P, CH * (TAPS + 3 + NST)])
        cw = chan[:, 0:CH * TAPS].rearrange("p (c k) -> p c k", c=CH)
        cb, bdt, dpw = (chan[:, CH * (TAPS + i):CH * (TAPS + i + 1)] for i in range(3))
        alog = chan[:, CH * (TAPS + 3):].rearrange("p (c n) -> p c n", c=CH)
        w_x = sb("w_x", [P, CH, P])
        w_dt = sb("w_dt", [P, DI])
        aneg = sb("aneg", [P, CH, NST])
        w_out = sb("w_out", [P, CH, D])

        xin = sb("xin", [P, TT, D])
        stat = sb("stat", [P, TT, 6])
        mv = sb("mv", [P, TT, 2])
        vare = sb("vare", [P, TT])
        rstd = sb("rstd", [P, TT])
        xn = sb("xn", [P, TT, D])
        xnT = sb("xnT", [P, HALF])
        xcp = sb("xcp", [P, CH, TAPS - 1 + HALF])
        cacc = sb("cacc", [P, CH, HALF])
        dlow = sb("dlow", [P, HALF])
        res1 = sb("res1", [32, HALF])
        mid0 = sb("mid0", [32, HALF], BF16)
        sp_abs = sb("sp_abs", [P, CH, HALF])
        sp_relu = sb("sp_relu", [P, CH, HALF])
        xc = sb("xc", [P, 2, CH, HALF])
        zs = sb("zs", [P, 2, CH, HALF])
        delta = sb("delta", [P, 2, CH, HALF])
        u = sb("u", [P, 2, CH, HALF])
        bcs = sb("bcs", [96, 2, HALF], BF16)
        hstate = sb("hstate", [P, (STEPS + SEQS) * NST * CH])
        ccarry = sb("ccarry", [P, STEPS + SEQS, CH, TAPS - 1])
        abuf = sb("abuf", [P, RING, CH, HALF])
        bx = sb("bx", [P, 2, CH, HALF])
        hbuf = sb("hbuf", [P, RING, CH, HALF])
        crep = sb("crep", [P, RING, HALF])
        cm = sb("cm", [P, RING, CH, HALF])
        xres = sb("xres", [P, TT, D])
        yd = sb("yd", [P, CH, HALF])
        yg = sb("yg", [P, CH, HALF])
        tstat = sb("tstat", [P, TT, 6])
        tmv = sb("tmv", [P, TT, 2])
        tvare = sb("tvare", [P, TT])
        trstd = sb("trstd", [P, TT])
        on = sb("on", [P, TT, D])
        x1t = sb("x1t", [P, TT, D])

        s_w = sem("weights_loaded")
        s_ident = sem("ident_made")
        s_sel = sem("sel_made")
        s_sel0 = sem("sel_cleared")
        s_consts = sem("constants_set")
        s_aexp = sem("a_exponentiated")
        s_aneg = sem("a_negated")
        s_xin = sem("xin_loaded")
        s_fstat = sem("front_stats")
        s_fvar = sem("front_variance")
        s_frstd = sem("front_rstd")
        s_xn = sem("xn_normed")
        s_tp = sem("xn_transposed")
        s_xnT = sem("xnT_copied")
        s_xcp_mm = sem("xc_projected")
        s_z_mm = sem("z_projected")
        s_xcp = sem("xcp_copied")
        s_cc = sem("carry_copied")
        s_tap0 = sem("tap0_done")
        s_tap = sem("taps_done")
        s_silu = sem("silu_done")
        s_dbc = sem("dbc_projected")
        s_hi = sem("bc_hi_split")
        s_dlow = sem("dlow_copied")
        s_res = sem("bc_residual")
        s_mid = sem("bc_mid_split")
        s_bcs = sem("bc_split")
        s_dt = sem("dt_projected")
        s_sp = sem("softplus_parts")
        s_spln = sem("softplus_log")
        s_delta = sem("delta_ready")
        s_u = sem("u_ready")
        s_brep = sem("b_spread")
        s_crep = sem("c_spread")
        s_a = sem("decay_ready")
        s_cs = sem("c_copied")
        s_bx = sem("bx_ready")
        s_scan = sem("scan_done")
        s_save = sem("state_saved")
        s_cm = sem("cm_ready")
        s_y = sem("y_summed")
        s_yd = sem("yd_ready")
        s_yg = sem("yg_ready")
        s_om = sem("out_projected")
        s_tstat = sem("tail_stats")
        s_tvar = sem("tail_variance")
        s_trstd = sem("tail_rstd")
        s_on = sem("out_normed")
        s_xres = sem("xres_loaded")
        s_x1 = sem("x1_ready")
        s_x1st = sem("x1_stored")

        block = ctx.enter_context(nc.Block())
        NW = 6

        x_t = x.rearrange("(g t p) d -> g p t d", t=TT, p=P)
        x1_t = x1.rearrange("(t a g l) d -> g t a l d", t=TT, a=P // 16, g=STEPS)

        def parity(g):
            return (g if isinstance(g, int) else g.guaranteed_mod_val) % 2

        def run_steps(part, engine):
            part(0, True, False)
            with engine.Fori(0, (STEPS - 2) // 2) as pair:
                part(pair * 2 + 1, False, False)
                part(pair * 2 + 2, False, False)
            part(STEPS - 1, False, True)

        @block.sync
        def _(sp):
            for dst, src in ((w_in[:, :], w_in_t),
                             (w_x[:, :, 0:32], w_x_t[:, RANK:RANK + 32].rearrange("(c p) r -> p c r", p=P)),
                             (w_x[:, :, 64:128], w_x_t[:, 0:RANK].rearrange("(c p) r -> p c r", p=P)),
                             (w_dt[64:128, :], w_dt_t),
                             (chan[:, :], per_channel),
                             (w_out[:, :, :], w_out_t.rearrange("(c p) d -> p c d", p=P))):
                sp.dma_start(dst, src).then_inc(s_w, 16)

            def load_x(f):
                sp.dma_start(xin[:, :, :], x_t[bass.ds(f, 1)].rearrange("o p t d -> (o p) t d")).then_inc(s_xin, 16)

            def store_x1(t):
                for j in range(TT):
                    sp.dma_start(x1_t[bass.ds(t, 1), j].rearrange("o a l d -> (o a) l d"),
                                 x1t[:, j, :]).then_inc(s_x1st, 16)

            def step(g):
                if not isinstance(g, int) or g + 2 < STEPS:
                    sp.wait_ge(s_xn, g + 2)
                    load_x(g + 2)
                if isinstance(g, int) and g == 0:
                    for dst, src in late_loads:
                        sp.dma_start(dst, src).then_inc(s_late, 16)
                else:
                    sp.wait_ge(s_x1, g)
                    store_x1(g - 1)
                sp.dma_start(xres[:, :, :], x_t[bass.ds(g, 1)].rearrange("o p t d -> (o p) t d")).then_inc(s_xres, 16)

            load_x(0)
            sp.wait_ge(s_xn, 1)
            load_x(1)
            step(0)
            with sp.Fori(1, STEPS - 2) as g:
                step(g)
            step(STEPS - 2)
            step(STEPS - 1)
            sp.wait_ge(s_x1, STEPS)
            store_x1(STEPS - 1)
            sp.wait_ge(s_x1st, 16 * TT * STEPS)
            sp.wait_ge(s_late, 16 * len(late_loads))

        @block.tensor
        def _(pe):
            def f_transpose(f):
                pe.wait_ge(s_xn, f + 1)
                if not isinstance(f, int) or f >= 1:
                    pe.wait_ge(s_sp, 2 * f)
                for t in range(TT):
                    mm = pe.transpose(m1[:, t * P:(t + 1) * P], xn[:, t, :], ident[:, :])
                mm.then_inc(s_tp, 1)

            def f_xc(f, c):
                if c == 0:
                    pe.wait_ge(s_xnT, f + 1)
                else:
                    pe.wait_ge(s_xcp, 2 * f + 1)
                pe.matmul(m1[:, :], w_in[:, c * P:(c + 1) * P], xnT[:, :],
                          start=True, stop=True).then_inc(s_xcp_mm, 1)

            def f_z(f, c):
                if c == 0:
                    pe.wait_ge(s_xcp, 2 * f + 2)
                elif not isinstance(f, int) or f >= 1:
                    pe.wait_ge(s_sp, 2 * f)
                    if not isinstance(f, int) or f >= 3:
                        pe.wait_ge(s_on, f - 2)
                pe.matmul((m1, m0)[c][:, :], w_in[:, DI + c * P:DI + (c + 1) * P], xnT[:, :],
                          start=True, stop=True).then_inc(s_z_mm, 1)

            def f_dbc(f):
                pe.wait_ge(s_silu, 4 * f + 4)
                for c in range(CH):
                    mm = pe.matmul(m1[:, :], w_x[:, c, :], xc[:, parity(f), c, :], start=c == 0, stop=c == CH - 1)
                mm.then_inc(s_dbc, 1)

            def f_dt(f, c):
                pe.wait_ge(s_dlow, f + 1)
                if c == 1:
                    pe.wait_ge(s_res, f + 1)
                pe.matmul((m0, m1)[c][:, :], w_dt[64:128, c * P:(c + 1) * P], dlow[64:128, :],
                          start=True, stop=True).then_inc(s_dt, 1)

            def spread(g, n):
                k = g * NST + n
                early = isinstance(g, int) and k < 2
                if n == 0:
                    pe.wait_ge(s_bcs, g + 1)
                if not early:
                    pe.wait_ge(s_bx, k - 1)
                rhs = bcs[:, parity(g), :]
                pe.matmul(ps_b[n % 2][:, :], sel[:, n, :], rhs, start=True, stop=True).then_inc(s_brep, 1)
                if not early:
                    pe.wait_ge(s_cs, k - 1)
                pe.matmul(ps_c[n % 2][:, :], sel[:, NST + n, :], rhs, start=True, stop=True).then_inc(s_crep, 1)

            def sum_state(g, n):
                pe.wait_ge(s_cm, g * NST + n + 1)
                if n == 0 and not (isinstance(g, int) and g == 0):
                    pe.wait_ge(s_yd, 2 * g)
                for c in range(CH):
                    mm = pe.matmul(ps_y[c][:, :], ident[:, :], cm[:, n % RING, c, :],
                                   start=n == 0, stop=n == NST - 1)
                mm.then_inc(s_y, 1)

            def t_project(t):
                pe.wait_ge(s_yg, t + 1)
                if isinstance(t, int) and t >= STEPS - 2:
                    pe.wait_ge(s_on, t)
                else:
                    pe.wait_ge(s_sp, 2 * t + 6)
                for j in range(TT):
                    for c in range(CH):
                        mm = pe.matmul(m0[:, j * P:(j + 1) * P], yg[:, c, j * P:(j + 1) * P], w_out[:, c, :],
                                       start=c == 0, stop=c == CH - 1)
                mm.then_inc(s_om, 1)

            def front_at(f, n):
                for at, part in ((1, lambda: f_transpose(f)), (2, lambda: f_xc(f, 0)), (3, lambda: f_xc(f, 1)),
                                 (4, lambda: f_z(f, 0)), (6, lambda: f_z(f, 1)), (8, lambda: f_dbc(f)),
                                 (10, lambda: f_dt(f, 0)), (11, lambda: f_dt(f, 1))):
                    if n == at:
                        part()

            def step(g, first, last):
                for n in range(NST):
                    if n < NST - 1:
                        spread(g, n + 1)
                    elif not last:
                        spread(g + 1, 0)
                    if not last:
                        front_at(g + 1, n)
                    if n >= 3:
                        sum_state(g, n - 3)
                    elif not first:
                        sum_state(g - 1, NST - 3 + n)
                    if n == TAIL_OUT and not first:
                        t_project(g - 1)

            pe.wait_ge(s_w, 16 * NW)
            pe.wait_ge(s_ident, 1)
            pe.wait_ge(s_sel, 1)
            for n in range(NST):
                front_at(0, n)
            spread(0, 0)
            run_steps(step, pe)
            for n in range(NST - 3, NST):
                sum_state(STEPS - 1, n)
            t_project(STEPS - 1)

        @block.scalar
        def _(act):
            def f_xnT(f):
                act.wait_ge(s_tp, f + 1)
                if not isinstance(f, int) or f >= 1:
                    act.wait_ge(s_z_mm, 2 * f)
                act.activation(xnT[:, :], m1[:, :], ACT.Copy).then_inc(s_xnT, 1)

            def f_xcp(f, c):
                act.wait_ge(s_xcp_mm, 2 * f + 1 + c)
                if not isinstance(f, int) or f >= 1:
                    act.wait_ge(s_tap, 6 * f)
                    act.wait_ge(s_cc, 2 * f)
                act.activation(xcp[:, c, TAPS - 1:], m1[:, :], ACT.Copy).then_inc(s_xcp, 1)

            def f_tap0(f, c):
                act.wait_ge(s_xcp, 2 * f + 1 + c)
                act.wait_ge(s_cc, 2 * f + 1)
                if not isinstance(f, int) or f >= 1:
                    act.wait_ge(s_silu, 4 * f)
                act.activation(cacc[:, c, :], xcp[:, c, 0:HALF], ACT.Identity,
                               bias=cb[:, c:c + 1], scale=cw[:, c, 0:1]).then_inc(s_tap0, 1)

            def f_silu(f):
                act.wait_ge(s_z_mm, 2 * f + 2)
                if not isinstance(f, int) or f >= 2:
                    act.wait_ge(s_yg, f - 1)
                    act.wait_ge(s_u, f - 1)
                for c in range(CH):
                    act.activation(zs[:, parity(f), c, :], (m1, m0)[c][:, :], ACT.Silu).then_inc(s_silu, 1)
                for c in range(CH):
                    act.wait_ge(s_tap, 6 * f + 5 + c)
                    act.activation(xc[:, parity(f), c, :], cacc[:, c, :], ACT.Silu).then_inc(s_silu, 1)
                act.preload_act_table_set(LN_SET)

            def f_split(f):
                bcf = bcs[:, parity(f), :]
                act.wait_ge(s_dbc, f + 1)
                if not isinstance(f, int) or f >= 2:
                    act.wait_ge(s_crep, (f - 1) * NST)
                act.activation(bcf[0:32, :], m1[0:32, :], ACT.Copy).then_inc(s_hi, 1)
                if not isinstance(f, int) or f >= 1:
                    act.wait_ge(s_dt, 2 * f)
                act.activation(dlow[64:128, :], m1[64:128, :], ACT.Copy).then_inc(s_dlow, 1)

            def f_mid(f):
                bcf = bcs[:, parity(f), :]
                act.wait_ge(s_res, f + 1)
                if not isinstance(f, int) or f >= 1:
                    act.wait_ge(s_bcs, f)
                act.activation(mid0[:, :], res1[:, :], ACT.Copy).then_inc(s_mid, 1)
                act.activation(bcf[32:64, :], res1[:, :], ACT.Copy).then_inc(s_mid, 1)

            def f_softplus(f, c):
                act.wait_ge(s_dt, 2 * f + 1 + c)
                if not isinstance(f, int) or f >= 1:
                    act.wait_ge(s_delta, f)
                act.activation(sp_abs[:, c, :], (m0, m1)[c][:, :], ACT.Abs, bias=bdt[:, c:c + 1])
                act.activation(sp_relu[:, c, :], (m0, m1)[c][:, :], ACT.Relu, bias=bdt[:, c:c + 1]).then_inc(s_sp, 1)

            def f_softlog(f):
                act.wait_ge(s_sp, 2 * f + 2)
                act.activation(sp_abs[:, :, :], sp_abs[:, :, :], ACT.Exp, scale=-1.0).then_inc(s_spln, 1)
                act.wait_ge(s_spln, 2 * f + 1)
                act.activation(sp_abs[:, :, :], sp_abs[:, :, :], ACT.Ln, bias=1.0).then_inc(s_spln, 1)

            def decay(g, n):
                k = g * NST + n
                if n == 0:
                    act.wait_ge(s_delta, g + 1)
                if not (isinstance(g, int) and k < RING):
                    act.wait_ge(s_scan, 2 * (k - RING + 1))
                for c in range(CH):
                    e = act.activation(abuf[:, n % RING, c, :], delta[:, parity(g), c, :], ACT.Exp,
                                       scale=aneg[:, c, n:n + 1])
                e.then_inc(s_a, 1)

            def c_copy(g, n):
                k = g * NST + n
                act.wait_ge(s_crep, k + 1)
                if not (isinstance(g, int) and k < RING):
                    act.wait_ge(s_cm, k - RING + 1)
                act.activation(crep[:, n % RING, :], ps_c[n % 2][:, :], ACT.Copy).then_inc(s_cs, 1)

            def front_at(f, n):
                for at, part in ((1, lambda: f_xnT(f)), (2, lambda: f_xcp(f, 0)), (3, lambda: f_xcp(f, 1)),
                                 (4, lambda: f_tap0(f, 0)), (5, lambda: f_tap0(f, 1)), (7, lambda: f_silu(f)),
                                 (8, lambda: f_split(f)), (9, lambda: f_mid(f)),
                                 (10, lambda: f_softplus(f, 0)), (11, lambda: f_softplus(f, 1)),
                                 (12, lambda: f_softlog(f))):
                    if n == at:
                        part()

            def step(g, first, last):
                for n in range(NST):
                    if n < NST - 1:
                        decay(g, n + 1)
                        c_copy(g, n + 1)
                    elif not last:
                        decay(g + 1, 0)
                        c_copy(g + 1, 0)
                    if not last:
                        front_at(g + 1, n)

            act.preload_act_table_set(LN_SET)
            act.wait_ge(s_w, 16 * NW)
            act.activation(aneg[:, :, :], alog, ACT.Exp).then_inc(s_aexp, 1)
            act.wait_ge(s_aexp, 1)
            act.activation(aneg[:, :, :], aneg[:, :, :], ACT.Copy, scale=-1.0).then_inc(s_aneg, 1)
            for n in range(NST):
                front_at(0, n)
            act.wait_ge(s_aneg, 1)
            decay(0, 0)
            c_copy(0, 0)
            run_steps(step, act)

        @block.vector
        def _(dve):
            def norm_stats(src, st, mean_var, s_bn, s_var, var_eps, count):
                for t in range(TT):
                    i = dve.bn_stats(st[:, t, :], src(t))
                i.then_inc(s_bn, 1)
                dve.wait_ge(s_bn, 2 * count + 1)
                dve.sem_inc(carrier, 1)
                dve.wait_ge(s_consts, 1)
                for t in range(TT):
                    i = dve.bn_aggr(mean_var[:, t, :], st[:, t, :])
                i.then_inc(s_bn, 1)
                dve.wait_ge(s_bn, 2 * count + 2)
                dve.tensor_scalar(var_eps[:, :], mean_var[:, :, 1], EPS, None, ALU.add).then_inc(s_var, 1)

            def f_stats(f):
                dve.wait_ge(s_xin, 16 * (f + 1))
                norm_stats(lambda t: xin[:, t, :], stat, mv, s_fstat, s_fvar, vare, f)

            def f_norm(f):
                dve.wait_ge(s_frstd, f + 1)
                if not isinstance(f, int) or f >= 1:
                    dve.wait_ge(s_tp, f)
                for t in range(TT):
                    i = dve.tensor_scalar(xn[:, t, :], xin[:, t, :], mv[:, t, 0:1], rstd[:, t:t + 1],
                                          ALU.subtract, ALU.mult)
                i.then_inc(s_xn, 1)

            def f_carry_in(f):
                if not isinstance(f, int) or f >= 1:
                    dve.wait_ge(s_tap0, 2 * f)
                    dve.wait_ge(s_tap, 6 * f)
                dve.wait_ge(s_cc, 2 * f)
                dve.tensor_copy(xcp[:, :, 0:TAPS - 1],
                                ccarry[:, bass.ds(f, 1), :, :].rearrange("p o c k -> p (o c) k")).then_inc(s_cc, 1)

            def f_carry_out(f):
                dve.wait_ge(s_xcp, 2 * f + 2)
                dve.tensor_copy(ccarry[:, bass.ds(f + SEQS, 1), :, :].rearrange("p o c k -> p (o c) k"),
                                xcp[:, :, HALF:]).then_inc(s_cc, 1)

            def f_tap(f, k):
                for c in range(CH):
                    if k == 1:
                        dve.wait_ge(s_tap0, 2 * f + 1 + c)
                    else:
                        dve.wait_ge(s_tap, 6 * f + 2 * (k - 2) + 1 + c)
                    dve.scalar_tensor_tensor(out=cacc[:, c, :], in0=xcp[:, c, k:k + HALF], scalar=cw[:, c, k:k + 1],
                                             in1=cacc[:, c, :], op0=ALU.mult, op1=ALU.add).then_inc(s_tap, 1)

            def f_res(f):
                bcf = bcs[:, parity(f), :]
                dve.wait_ge(s_hi, f + 1)
                if not isinstance(f, int) or f >= 1:
                    dve.wait_ge(s_mid, 2 * f)
                    dve.wait_ge(s_bcs, f)
                dve.tensor_tensor(res1[:, :], m1[0:32, :], bcf[0:32, :], ALU.subtract).then_inc(s_res, 1)

            def f_lo(f):
                bcf = bcs[:, parity(f), :]
                dve.wait_ge(s_mid, 2 * f + 2)
                dve.tensor_tensor(bcf[64:96, :], res1[:, :], mid0[:, :], ALU.subtract).then_inc(s_bcs, 1)

            def f_delta(f):
                dve.wait_ge(s_spln, 2 * f + 2)
                if not isinstance(f, int) or f >= 2:
                    dve.wait_ge(s_a, (f - 1) * NST)
                    dve.wait_ge(s_u, f - 1)
                dve.tensor_tensor(delta[:, parity(f), :, :], sp_abs[:, :, :], sp_relu[:, :, :], ALU.add).then_inc(s_delta, 1)

            def make_bx(g, n):
                k = g * NST + n
                if n == 0:
                    dve.wait_ge(s_u, g + 1)
                dve.wait_ge(s_brep, k + 1)
                if not (isinstance(g, int) and k < 2):
                    dve.wait_ge(s_scan, 2 * (k - 1))
                b = ps_b[n % 2][:, :].unsqueeze(1).broadcast_to([P, CH, HALF])
                dve.tensor_tensor(bx[:, n % 2, :, :], u[:, parity(g), :, :], b, ALU.mult).then_inc(s_bx, 1)

            def scan(g, n):
                k = g * NST + n
                dve.wait_ge(s_a, k + 1)
                dve.wait_ge(s_bx, k + 1)
                if not (isinstance(g, int) and k < RING):
                    dve.wait_ge(s_cm, k - RING + 1)
                    dve.wait_ge(s_save, k - RING + 1)
                for c in range(CH):
                    dve.tensor_tensor_scan(hbuf[:, n % RING, c, :], abuf[:, n % RING, c, :], bx[:, n % 2, c, :],
                                           hstate[:, bass.ds(g * (NST * CH) + n * CH + c, 1)],
                                           ALU.mult, ALU.add).then_inc(s_scan, 1)

            def save(g, n):
                k = g * NST + n
                dve.wait_ge(s_scan, 2 * k + 2)
                dve.tensor_copy(hstate[:, bass.ds((g + SEQS) * (NST * CH) + n * CH, CH)],
                                hbuf[:, n % RING, :, HALF - 1]).then_inc(s_save, 1)

            def t_skip(t):
                dve.wait_ge(s_y, (t + 1) * NST)
                if not isinstance(t, int) or t >= 1:
                    dve.wait_ge(s_yg, t)
                for c in range(CH):
                    dve.scalar_tensor_tensor(out=yd[:, c, :], in0=xc[:, parity(t), c, :], scalar=dpw[:, c:c + 1],
                                             in1=ps_y[c][:, :], op0=ALU.mult, op1=ALU.add).then_inc(s_yd, 1)

            def t_gate(t):
                dve.wait_ge(s_yd, 2 * t + 2)
                if not isinstance(t, int) or t >= 1:
                    dve.wait_ge(s_om, t)
                dve.tensor_tensor(yg[:, :, :], yd[:, :, :], zs[:, parity(t), :, :], ALU.mult).then_inc(s_yg, 1)

            def t_stats(t):
                dve.wait_ge(s_om, t + 1)
                norm_stats(lambda j: m0[:, j * P:(j + 1) * P], tstat, tmv, s_tstat, s_tvar, tvare, t)

            def t_norm(t):
                dve.wait_ge(s_trstd, t + 1)
                if not isinstance(t, int) or t >= 1:
                    dve.wait_ge(s_x1, t)
                for j in range(TT):
                    i = dve.tensor_scalar(on[:, j, :], m0[:, j * P:(j + 1) * P], tmv[:, j, 0:1], trstd[:, j:j + 1],
                                          ALU.subtract, ALU.mult)
                i.then_inc(s_on, 1)

            def front_at(f, n):
                for at, part in ((0, lambda: f_stats(f)), (1, lambda: f_norm(f)), (2, lambda: f_carry_in(f)),
                                 (4, lambda: f_tap(f, 1)), (5, lambda: f_tap(f, 2)), (6, lambda: f_tap(f, 3)),
                                 (7, lambda: f_carry_out(f)), (8, lambda: f_res(f)), (9, lambda: f_lo(f)),
                                 (13, lambda: f_delta(f))):
                    if n == at:
                        part()

            def step(g, first, last):
                for n in range(NST):
                    make_bx(g, n)
                    if n >= 1:
                        scan(g, n - 1)
                    elif not first:
                        scan(g - 1, NST - 1)
                    if n >= 2:
                        save(g, n - 2)
                    elif not first:
                        save(g - 1, NST - 2 + n)
                    if not last:
                        front_at(g + 1, n)
                    if not first:
                        if n == TAIL_SKIP:
                            t_skip(g - 1)
                            t_gate(g - 1)
                        if n == TAIL_OUT + 1:
                            t_stats(g - 1)
                        if n == TAIL_OUT + 2:
                            t_norm(g - 1)

            dve.memset(w_x[:, :, 32:64], 0.0)
            dve.memset(hstate[:, 0:SEQS * NST * CH], 0.0)
            dve.memset(half_neg[:, :], -0.5)
            dve.memset(ccarry[:, 0:SEQS, :, :], 0.0).then_inc(s_consts, 1)
            dve.wait_ge(s_consts, 1)
            dve.wait_ge(s_w, 16 * NW)
            for n in range(NST):
                front_at(0, n)
            run_steps(step, dve)
            scan(STEPS - 1, NST - 1)
            save(STEPS - 1, NST - 2)
            save(STEPS - 1, NST - 1)
            t_skip(STEPS - 1)
            t_gate(STEPS - 1)
            t_stats(STEPS - 1)
            t_norm(STEPS - 1)

        @block.gpsimd
        def _(pool):
            pool.memset(sel[:, :, :], 0.0).then_inc(s_sel0, 1)
            pool.memset(ident[:, :], 0.0).then_inc(s_sel0, 1)
            pool.wait_ge(s_sel0, 2)
            pool.affine_select(out=ident[:, :], in_=ident[:, :], compare_op=ALU.not_equal, fill=1.0, base=0,
                               pattern=[[-1, P]], channel_multiplier=1).then_inc(s_ident, 1)
            for part in range(3):
                pool.affine_select(out=sel[:, :, :], in_=sel[:, :, :], compare_op=ALU.not_equal, fill=1.0,
                                   base=-32 * part, pattern=[[-1, 2 * NST], [0, P]],
                                   channel_multiplier=1).then_inc(s_sel0, 1)
                pool.wait_ge(s_sel0, 3 + part)
            pool.sem_inc(s_sel, 1)

            def f_rstd(f):
                pool.wait_ge(s_fvar, f + 1)
                pool.tensor_tensor(rstd[:, :], vare[:, :], half_neg[:, :], ALU.pow).then_inc(s_frstd, 1)

            def f_u(f):
                pool.wait_ge(s_delta, f + 1)
                if not isinstance(f, int) or f >= 2:
                    pool.wait_ge(s_bx, (f - 1) * NST)
                pool.tensor_tensor(u[:, parity(f), :, :], delta[:, parity(f), :, :], xc[:, parity(f), :, :], ALU.mult).then_inc(s_u, 1)

            def product(g, n):
                k = g * NST + n
                pool.wait_ge(s_scan, 2 * k + 2)
                pool.wait_ge(s_cs, k + 1)
                if not (isinstance(g, int) and k < RING):
                    pool.wait_ge(s_y, k - RING + 1)
                c = crep[:, n % RING, :].unsqueeze(1).broadcast_to([P, CH, HALF])
                pool.tensor_tensor(cm[:, n % RING, :, :], hbuf[:, n % RING, :, :], c, ALU.mult).then_inc(s_cm, 1)

            def t_rstd(t):
                pool.wait_ge(s_tvar, t + 1)
                pool.tensor_tensor(trstd[:, :], tvare[:, :], half_neg[:, :], ALU.pow).then_inc(s_trstd, 1)

            def t_add(t):
                pool.wait_ge(s_on, t + 1)
                pool.wait_ge(s_xres, 16 * (t + 1))
                if not isinstance(t, int) or t >= 1:
                    pool.wait_ge(s_x1st, 16 * TT * t)
                pool.tensor_tensor(x1t[:, :, :], on[:, :, :], xres[:, :, :], ALU.add).then_inc(s_x1, 1)

            def step(g, first, last):
                for n in range(NST):
                    if not last and n == 0:
                        f_rstd(g + 1)
                    if not first and n == TAIL_OUT + 1:
                        t_rstd(g - 1)
                    if not first and n == TAIL_OUT + 2:
                        t_add(g - 1)
                    if not last and n == 13:
                        f_u(g + 1)
                    if n >= 1:
                        product(g, n - 1)
                    elif not first:
                        product(g - 1, NST - 1)

            pool.wait_ge(s_consts, 1)
            f_rstd(0)
            f_u(0)
            run_steps(step, pool)
            product(STEPS - 1, NST - 1)
            t_rstd(STEPS - 1)
            t_add(STEPS - 1)
GROUPS, GT = 16, 4
POS = 16
CAP = SEQS * LENGTH + P
ROW = 2 * D + 1
QUADS = 18
TILES = 4 * QUADS
SCALE = HD ** -0.5
MASKED = -1e30


def attention(nc, sem, carrier, banks, ident, half_neg, w, shared, x1, routed):
    ctx = ExitStack()

    def sb(name, shape, dt=F32):
        return ctx.enter_context(nc.sbuf_tensor(name, shape, dt))

    with ctx:
        ps_s, ps_t, ps_o, ps_ot = banks[0:2], banks[2], banks[3], banks[4]
        ps_p, ps_a, ps_l = banks[5], banks[6], banks[7]

        mask_l = sb("mask_l", [POS, P], BF16)
        mask_r = sb("mask_r", [POS, HEADS, P], BF16)
        before = sb("before", [P, P], BF16)
        ones = sb("ones", [P, P], BF16)
        xg = sb("xg", [P, 2, GT, D])
        xn = sb("b_xn", [P, 2, GT, D])
        stat = sb("b_stat", [P, GT, 6])
        mv = sb("b_mv", [P, GT, 2])
        vare = sb("b_vare", [P, GT])
        rstd = sb("b_rstd", [P, GT])
        xT = sb("b_xT", [P, GT * P])
        qT = sb("qT", [P, 2, GT * P])
        kz = sb("kz", [P, 2, GT, HEADS, P])
        va = sb("va", [P, 2, GT, HEADS, HD + 1])
        xb = sb("xb", [P, 2, GT, D])
        mx = sb("mx", [P, 2, HEADS])
        sub = sb("sub", [P, 2, HEADS, P])
        pr = sb("pr", [P, 2, HEADS, P])
        pT = sb("pT", [P, 2, HEADS, P])
        rs = sb("rs", [P, 2, HEADS])
        o = sb("o", [P, 2, HEADS, HD])
        oT = sb("oT", [P, 2, P])
        r1 = sb("r1", [P, GT, D])
        stat1 = sb("b_stat1", [P, GT, 6])
        mv1 = sb("b_mv1", [P, GT, 2])
        vare1 = sb("b_vare1", [P, GT])
        rstd1 = sb("b_rstd1", [P, GT])
        yn = sb("yn", [P, GT, D])
        yg = sb("yg1", [P, GT, D])
        pk = sb("pk", [P, 2, GT, ROW])
        yT = sb("yT", [P, GT * P])
        lmax = sb("lmax", [P, GT])
        eq = sb("eq", [P, GT, EXPERTS])
        eqr = sb("eqr", [P, GT, EXPERTS])
        rmax = sb("rmax", [P, GT])
        hot = sb("hot", [P, GT, EXPERTS])
        hot_h = sb("hot_h", [P, GT, EXPERTS], BF16)
        cum = sb("cum", [P, GT + 1, EXPERTS])
        cum_h = sb("cum_h", [P, GT, EXPERTS], BF16)
        pose = sb("pose", [P, GT, EXPERTS])
        dest = sb("dest", [P, GT])
        desti = sb("desti", [P, 2, GT], I32)
        cnt = sb("cnt", [P, EXPERTS])
        more = sb("more", [P, EXPERTS, SEQS * LENGTH // P])
        tiles = sb("tiles", [P, EXPERTS])
        tend = sb("tend", [P, EXPERTS])
        onesr = sb("onesr", [P, EXPERTS])
        full = sb("full", [P, TILES, EXPERTS])
        part = sb("part", [P, TILES, EXPERTS])
        te = sb("te", [P, TILES])
        tfirst = sb("tfirst", [P, TILES])
        trow = sb("trow", [P, TILES])
        live = sb("live", [P, TILES])
        bres = sb("bias_residual", [EXPERTS, DF + D])
        bmid = sb("bias_mid", [EXPERTS, DF + D], BF16)
        padrow = sb("padrow", [P, ROW])
        padi = sb("padi", [P, EXPERTS + 1], I32)
        padf = sb("padf", [P, EXPERTS + 1])

        names = """masks_cleared masks_made kz_cleared xg_loaded0 xg_loaded1 b_stats b_variance b_rstd b_normed b_transposed
            xT_copied q_projected k_projected q_copied k_copied v_projected v_copied xb_ready scores max_found max_subtracted
            probs_ready probs_transposed pT_copied values_summed sums_inverted o_ready o_transposed oT_copied
            attn_projected r1_ready r1_stats r1_variance r1_rstd r1_normed y_scaled y_ready pk_x1_loaded0 pk_x1_loaded1 y_transposed
            yT_copied logits_ready route_chain one_hot cum_ready ranks_counted dest_ready row_ids rows_scattered0 rows_scattered1
            counts_ready bias_chain table_chain pad_indices pad_row pad_scattered"""
        S = {n: sem("B_" + n) for n in names.split()}

        x1_g = x1.rearrange("(j w p) d -> j p w d", w=GT, p=P)

        def parity(j):
            return (j if isinstance(j, int) else j.guaranteed_mod_val) % 2

        def loads(j):
            return 8 * (j - parity(j)) + 16

        def past(j, n):
            if isinstance(j, int):
                return j >= n
            assert j.min_val >= n, "peel more groups"
            return True

        def at_most(count, limit):
            return min(count, limit) if isinstance(count, int) else count

        def run_slots(slot, engine):
            for j in range(-1, 5):
                slot(j)
            with engine.Fori(2, GROUPS // 2 - 1) as pair:
                slot(pair * 2 + 1)
                slot(pair * 2 + 2)
            for j in range(GROUPS - 1, GROUPS + 3):
                slot(j)

        def has(j):
            return not isinstance(j, int) or 0 <= j < GROUPS

        def lagged(part, j, i, lag):
            j, i = (j, i - lag) if i >= lag else (j - 1, i - lag + GT)
            if has(j):
                part(j, i)

        block = ctx.enter_context(nc.Block())

        @block.sync
        def _(sp):
            def load_x(j):
                if past(j, 2):
                    sp.wait_ge(S["b_normed"], j - 1)
                    sp.sem_inc(carrier, 1)
                    sp.wait_ge(S["b_stats"], 2 * (j - 1))
                    sp.sem_inc(carrier, 1)
                sp.dma_start(xg[:, parity(j), :, :], x1_g[bass.ds(j, 1)].rearrange("o p w d -> (o p) w d"))\
                  .then_inc(S[f"xg_loaded{parity(j)}"], 16)

            def load_pk(j):
                if past(j, 2):
                    sp.wait_ge(S[f"rows_scattered{parity(j)}"], 8 * GT * (j - parity(j)))
                    sp.sem_inc(carrier, 1)
                sp.dma_start(pk[:, parity(j), :, D:2 * D], x1_g[bass.ds(j, 1)].rearrange("o p w d -> (o p) w d"))\
                  .then_inc(S[f"pk_x1_loaded{parity(j)}"], 16)

            def slot(j):
                if has(j + 1):
                    load_x(j + 1)
                if has(j - 2):
                    load_pk(j - 2)

            run_slots(slot, sp)

        @block.tensor
        def _(pe):
            def b_transpose(j):
                pe.wait_ge(S["b_normed"], j + 1)
                if past(j, 1):
                    pe.wait_ge(S["v_copied"], j)
                if past(j, 4):
                    pe.wait_ge(S["yT_copied"], j - 3)
                for w_ in range(GT):
                    mm = pe.transpose(ps_a[:, w_ * P:(w_ + 1) * P], xn[:, parity(j), w_, :], ident[:, :])
                mm.then_inc(S["b_transposed"], 1)

            def project_q(j):
                pe.wait_ge(S["xT_copied"], j + 1)
                pe.matmul(ps_a[:, :], w["wqk"][:, 0:D], xT[:, :], start=True, stop=True).then_inc(S["q_projected"], 1)

            def project_k(j):
                pe.wait_ge(S["q_copied"], j + 1)
                pe.matmul(ps_a[:, :], w["wqk"][:, D:2 * D], xT[:, :], start=True, stop=True)\
                  .then_inc(S["k_projected"], 1)

            def project_v(j):
                pe.wait_ge(S["k_copied"], HEADS * (j + 1))
                for w_ in range(GT):
                    mm = pe.matmul(ps_a[:, w_ * D:(w_ + 1) * D], xT[:, w_ * P:(w_ + 1) * P], w["wqk"][:, 2 * D:3 * D],
                                   start=True, stop=True)
                mm.then_inc(S["v_projected"], 1)

            def scores(j, i):
                tile = j * GT + i
                if i == 0:
                    pe.wait_ge(S["k_copied"], HEADS * (j + 1))
                if not isinstance(j, int) or j * GT + i >= 2:
                    pe.wait_ge(S["max_subtracted"], tile - 1)
                pe.matmul(ps_s[i % 2][:, :], qT[:, parity(j), i * P:(i + 1) * P], kz[:, parity(j), i, :, :],
                          start=True, stop=False)
                pe.matmul(ps_s[i % 2][:, :], mask_l[:, :], mask_r[:, :, :], start=False, stop=True)\
                  .then_inc(S["scores"], 1)

            def turn_probs(j, i):
                tile = j * GT + i
                pe.wait_ge(S["probs_ready"], tile + 1)
                if not isinstance(j, int) or j * GT + i >= 1:
                    pe.wait_ge(S["pT_copied"], tile)
                for h in range(HEADS):
                    mm = pe.transpose(ps_t[:, h * P:(h + 1) * P], pr[:, i % 2, h, :], ident[:, :])
                mm.then_inc(S["probs_transposed"], 1)

            def sum_values(j, i):
                tile = j * GT + i
                pe.wait_ge(S["pT_copied"], tile + 1)
                if i == 0:
                    pe.wait_ge(S["v_copied"], j + 1)
                if not isinstance(j, int) or j * GT + i >= 1:
                    pe.wait_ge(S["o_ready"], tile)
                for h in range(HEADS):
                    mm = pe.matmul(ps_o[:, h * (HD + 1):(h + 1) * (HD + 1)], pT[:, i % 2, h, :],
                                   va[:, parity(j), i, h, :], start=True, stop=True)
                mm.then_inc(S["values_summed"], 1)

            def turn_o(j, i):
                tile = j * GT + i
                pe.wait_ge(S["o_ready"], tile + 1)
                if not isinstance(j, int) or j * GT + i >= 1:
                    pe.wait_ge(S["oT_copied"], tile)
                pe.transpose(ps_ot[:, 0:P], o[:, i % 2, :, :].rearrange("p h e -> p (h e)"), ident[:, :])\
                  .then_inc(S["o_transposed"], 1)

            def project_o(j, i):
                pe.wait_ge(S["oT_copied"], j * GT + i + 1)
                if i == 0 and past(j, 1):
                    pe.wait_ge(S["r1_ready"], j)
                pe.matmul(ps_p[:, i * D:(i + 1) * D], oT[:, i % 2, :], w["wo"][:, :], start=True, stop=True)\
                  .then_inc(S["attn_projected"], 1)

            def turn_y(j):
                pe.wait_ge(S["y_ready"], j + 1)
                pe.wait_ge(S["v_copied"], at_most(j + 4, GROUPS))
                for w_ in range(GT):
                    mm = pe.transpose(ps_a[:, w_ * P:(w_ + 1) * P], pk[:, parity(j), w_, 0:D], ident[:, :])
                mm.then_inc(S["y_transposed"], 1)

            def logits(j):
                pe.wait_ge(S["yT_copied"], j + 1)
                if past(j, 1):
                    pe.wait_ge(S["dest_ready"], j)
                for w_ in range(GT):
                    mm = pe.matmul(ps_l[:, w_ * EXPERTS:(w_ + 1) * EXPERTS], yT[:, w_ * P:(w_ + 1) * P], w["wg"][:, :],
                                   start=True, stop=True)
                mm.then_inc(S["logits_ready"], 1)

            def ranks(j):
                pe.wait_ge(S["cum_ready"], j + 1)
                pe.matmul(ps_l[:, 64:64 + GT * EXPERTS], before[:, :], hot_h[:, :, :], start=True, stop=False)
                pe.matmul(ps_l[:, 64:64 + GT * EXPERTS], ones[:, :], cum_h[:, :, :], start=False, stop=True)\
                  .then_inc(S["ranks_counted"], 1)

            def slot(j):
                for s in range(GT):
                    if has(j):
                        scores(j, s)
                    if s == 0 and has(j - 3):
                        turn_y(j - 3)
                    if s == 1 and has(j - 3):
                        logits(j - 3)
                    lagged(turn_probs, j, s, 1)
                    if s == 2 and has(j + 1):
                        project_q(j + 1)
                    if s == 2 and has(j - 3):
                        ranks(j - 3)
                    lagged(sum_values, j, s, 2)
                    lagged(turn_o, j, s, 3)
                    lagged(project_o, j, s, 4)
                    if s == 3 and has(j + 1):
                        project_v(j + 1)
                    if s == 1 and has(j + 1):
                        b_transpose(j + 1)
                    if s == 2 and has(j + 1):
                        project_k(j + 1)

            pe.wait_ge(S["masks_made"], 4)
            run_slots(slot, pe)
            pe.wait_ge(S["cum_ready"], GROUPS + 1)
            pe.wait_ge(S["dest_ready"], GROUPS)
            pe.matmul(ps_l[:, 0:EXPERTS], ones[:, :], cum_h[:, 0, :], start=True, stop=True)\
              .then_inc(S["counts_ready"], 1)

        @block.scalar
        def _(act):
            def copy_xT(j):
                act.wait_ge(S["b_transposed"], j + 1)
                if past(j, 1):
                    act.wait_ge(S["v_projected"], j)
                act.activation(xT[:, :], ps_a[:, :], ACT.Copy).then_inc(S["xT_copied"], 1)

            def copy_q(j):
                act.wait_ge(S["q_projected"], j + 1)
                if past(j, 2):
                    act.wait_ge(S["scores"], GT * (j - 1))
                act.activation(qT[:, parity(j), :], ps_a[:, :], ACT.Identity, bias=w["bqk"][:, 0:1])\
                   .then_inc(S["q_copied"], 1)

            def copy_k(j):
                act.wait_ge(S["k_projected"], j + 1)
                for h in range(HEADS):
                    r = slice(h * HD, (h + 1) * HD)
                    act.activation(kz[r, parity(j), :, h, :], ps_a[r, :].rearrange("p (w k) -> p w k", w=GT),
                                   ACT.Identity, bias=w["bqk"][r, 1:2]).then_inc(S["k_copied"], 1)

            def exponent(j, i):
                tile = j * GT + i
                act.wait_ge(S["max_subtracted"], tile + 1)
                if not isinstance(j, int) or j * GT + i >= 2:
                    act.wait_ge(S["probs_transposed"], tile - 1)
                act.activation(pr[:, i % 2, :, :], sub[:, i % 2, :, :], ACT.Exp, scale=SCALE)\
                   .then_inc(S["probs_ready"], 1)

            def copy_pT(j, i):
                tile = j * GT + i
                act.wait_ge(S["probs_transposed"], tile + 1)
                if not isinstance(j, int) or j * GT + i >= 2:
                    act.wait_ge(S["values_summed"], tile - 1)
                act.activation(pT[:, i % 2, :, :], ps_t[:, :].rearrange("p (h q) -> p h q", h=HEADS), ACT.Copy)\
                   .then_inc(S["pT_copied"], 1)

            def copy_oT(j, i):
                tile = j * GT + i
                act.wait_ge(S["o_transposed"], tile + 1)
                if not isinstance(j, int) or j * GT + i >= 2:
                    act.wait_ge(S["attn_projected"], tile - 1)
                act.activation(oT[:, i % 2, :], ps_ot[:, 0:P], ACT.Copy).then_inc(S["oT_copied"], 1)

            def copy_yT(j):
                act.wait_ge(S["y_transposed"], j + 1)
                if past(j, 1):
                    act.wait_ge(S["logits_ready"], j)
                act.activation(yT[:, :], ps_a[:, :], ACT.Copy).then_inc(S["yT_copied"], 1)

            def slot(j):
                for s in range(GT):
                    if has(j):
                        exponent(j, s)
                    if s == 0 and has(j - 3):
                        copy_yT(j - 3)
                    lagged(copy_pT, j, s, 1)
                    if s == 2 and has(j + 1):
                        copy_q(j + 1)
                    lagged(copy_oT, j, s, 3)
                    if s == 2 and has(j + 1):
                        copy_k(j + 1)
                    if s == 1 and has(j + 1):
                        copy_xT(j + 1)

            act.wait_ge(S["kz_cleared"], 1)
            run_slots(slot, act)

        @block.vector
        def _(dve):
            def stats(src, st, mean_var, s_bn, s_var, var_eps, j):
                for t in range(GT):
                    i = dve.bn_stats(st[:, t, :], src(t))
                i.then_inc(s_bn, 1)
                dve.wait_ge(s_bn, 2 * j + 1)
                dve.sem_inc(carrier, 1)
                for t in range(GT):
                    i = dve.bn_aggr(mean_var[:, t, :], st[:, t, :])
                i.then_inc(s_bn, 1)
                dve.wait_ge(s_bn, 2 * j + 2)
                dve.tensor_scalar(var_eps[:, :], mean_var[:, :, 1], EPS, None, ALU.add).then_inc(s_var, 1)

            def b_stats(j):
                dve.wait_ge(S[f"xg_loaded{parity(j)}"], loads(j))
                stats(lambda t: xg[:, parity(j), t, :], stat, mv, S["b_stats"], S["b_variance"], vare, j)

            def b_norm(j):
                dve.wait_ge(S["b_rstd"], j + 1)
                if past(j, 2):
                    dve.wait_ge(S["b_transposed"], j - 1)
                    dve.wait_ge(S["xb_ready"], j - 1)
                for t in range(GT):
                    i = dve.tensor_scalar(xn[:, parity(j), t, :], xg[:, parity(j), t, :], mv[:, t, 0:1],
                                          rstd[:, t:t + 1], ALU.subtract, ALU.mult)
                i.then_inc(S["b_normed"], 1)

            def copy_v(j):
                dve.wait_ge(S["v_projected"], j + 1)
                if past(j, 2):
                    dve.wait_ge(S["values_summed"], GT * (j - 1))
                bias = w["rows"][:, 0, :].rearrange("p (h e) -> p h e", h=HEADS).unsqueeze(1)
                dve.tensor_tensor(va[:, parity(j), :, :, 0:HD],
                                  ps_a[:, :].rearrange("p (w h e) -> p w h e", w=GT, h=HEADS),
                                  bias.broadcast_to([P, GT, HEADS, HD]), ALU.add).then_inc(S["v_copied"], 1)

            def less_max(j, i):
                tile = j * GT + i
                sc = ps_s[i % 2][:, :].rearrange("p (h k) -> p h k", h=HEADS)
                dve.wait_ge(S["scores"], tile + 1)
                dve.tensor_reduce(mx[:, i % 2, :], sc, AX.X, ALU.max).then_inc(S["max_found"], 1)
                if not isinstance(j, int) or j * GT + i >= 2:
                    dve.wait_ge(S["probs_ready"], tile - 1)
                dve.wait_ge(S["max_found"], tile + 1)
                dve.tensor_tensor(sub[:, i % 2, :, :], sc, mx[:, i % 2, :].unsqueeze(2).broadcast_to([P, HEADS, P]),
                                  ALU.subtract).then_inc(S["max_subtracted"], 1)

            def norm_o(j, i):
                tile = j * GT + i
                po = ps_o[:, 0:HEADS * (HD + 1)].rearrange("p (h e) -> p h e", h=HEADS)
                dve.wait_ge(S["values_summed"], tile + 1)
                dve.reciprocal(rs[:, i % 2, :], po[:, :, HD]).then_inc(S["sums_inverted"], 1)
                if not isinstance(j, int) or j * GT + i >= 2:
                    dve.wait_ge(S["o_transposed"], tile - 1)
                dve.wait_ge(S["sums_inverted"], tile + 1)
                dve.tensor_tensor(o[:, i % 2, :, :], po[:, :, 0:HD],
                                  rs[:, i % 2, :].unsqueeze(2).broadcast_to([P, HEADS, HD]), ALU.mult)\
                   .then_inc(S["o_ready"], 1)

            def residual(j):
                dve.wait_ge(S["attn_projected"], GT * (j + 1))
                dve.wait_ge(S["xb_ready"], j + 1)
                if past(j, 1):
                    dve.wait_ge(S["r1_normed"], j)
                dve.tensor_tensor(r1[:, :, :], ps_p[:, :].rearrange("p (w d) -> p w d", w=GT), xb[:, parity(j), :, :],
                                  ALU.add).then_inc(S["r1_ready"], 1)
                dve.wait_ge(S["r1_ready"], j + 1)
                stats(lambda t: r1[:, t, :], stat1, mv1, S["r1_stats"], S["r1_variance"], vare1, j)

            def norm1(j):
                dve.wait_ge(S["r1_rstd"], j + 1)
                if past(j, 1):
                    dve.wait_ge(S["y_scaled"], j)
                for t in range(GT):
                    i = dve.tensor_scalar(yn[:, t, :], r1[:, t, :], mv1[:, t, 0:1], rstd1[:, t:t + 1],
                                          ALU.subtract, ALU.mult)
                i.then_inc(S["r1_normed"], 1)

            def choose(j):
                lg = ps_l[:, 0:GT * EXPERTS].rearrange("p (w e) -> p w e", w=GT)
                chain, c = S["route_chain"], 5
                dve.wait_ge(S["logits_ready"], j + 1)
                if past(j, 1):
                    dve.wait_ge(S["dest_ready"], j)
                dve.tensor_reduce(lmax[:, :], lg, AX.X, ALU.max).then_inc(chain, 1)
                dve.wait_ge(chain, c * j + 1)
                dve.tensor_tensor(eq[:, :, :], lg, lmax[:, :].unsqueeze(2).broadcast_to([P, GT, EXPERTS]), ALU.is_equal)\
                   .then_inc(chain, 1)
                dve.wait_ge(chain, c * j + 2)
                order = shared["order"][:, :].unsqueeze(1).broadcast_to([P, GT, EXPERTS])
                dve.tensor_tensor(eqr[:, :, :], eq[:, :, :], order, ALU.mult).then_inc(chain, 1)
                dve.wait_ge(chain, c * j + 3)
                dve.tensor_reduce(rmax[:, :], eqr[:, :, :], AX.X, ALU.max).then_inc(chain, 1)
                dve.wait_ge(chain, c * j + 4)
                dve.tensor_tensor(hot[:, :, :], eqr[:, :, :], rmax[:, :].unsqueeze(2).broadcast_to([P, GT, EXPERTS]),
                                  ALU.is_equal).then_inc(chain, 1)
                dve.wait_ge(chain, c * j + 5)
                if past(j, 1):
                    dve.wait_ge(S["ranks_counted"], j)
                dve.tensor_copy(hot_h[:, :, :], hot[:, :, :])
                for t in range(GT):
                    dve.tensor_tensor(cum[:, t + 1, :], cum[:, t, :], hot[:, t, :], ALU.add)\
                       .then_inc(S["one_hot"], 1)
                    dve.wait_ge(S["one_hot"], (GT + 2) * j + t + 1)
                dve.tensor_copy(cum_h[:, :, :], cum[:, 0:GT, :]).then_inc(S["one_hot"], 1)
                dve.wait_ge(S["one_hot"], (GT + 2) * j + GT + 1)
                dve.tensor_copy(cum[:, 0, :], cum[:, GT, :]).then_inc(S["one_hot"], 1)
                dve.wait_ge(S["one_hot"], (GT + 2) * j + GT + 2)
                dve.sem_inc(S["cum_ready"], 1)

            def place(j):
                if past(j, 1):
                    dve.wait_ge(S["dest_ready"], j)
                dve.wait_ge(S["ranks_counted"], j + 1)
                dve.tensor_tensor(pose[:, :, :], ps_l[:, 64:64 + GT * EXPERTS].rearrange("p (w e) -> p w e", w=GT),
                                  shared["region"][:, :].unsqueeze(1).broadcast_to([P, GT, EXPERTS]), ALU.add)\
                   .then_inc(S["row_ids"], 1)
                dve.wait_ge(S["row_ids"], 5 * j + 1)
                dve.tensor_tensor(pose[:, :, :], pose[:, :, :], hot[:, :, :], ALU.mult).then_inc(S["row_ids"], 1)
                dve.wait_ge(S["row_ids"], 5 * j + 2)
                dve.tensor_reduce(dest[:, :], pose[:, :, :], AX.X, ALU.add).then_inc(S["row_ids"], 1)
                dve.wait_ge(S["row_ids"], 5 * j + 3)
                if past(j, 2):
                    dve.wait_ge(S[f"rows_scattered{parity(j)}"], 8 * GT * (j - parity(j)))
                dve.tensor_copy(desti[:, parity(j), :], dest[:, :]).then_inc(S["row_ids"], 1)
                dve.tensor_copy(pk[:, parity(j), :, 2 * D].bitcast(I32), shared["ids"][:, bass.ds(j * GT, GT)])\
                   .then_inc(S["row_ids"], 1)
                dve.wait_ge(S["row_ids"], 5 * j + 5)
                dve.sem_inc(S["dest_ready"], 1)

            def slot(j):
                for s in range(GT):
                    if has(j):
                        less_max(j, s)
                    if s == 0 and has(j + 1):
                        b_stats(j + 1)
                    if s == 0 and has(j - 2):
                        residual(j - 2)
                    if s == 1 and has(j + 1):
                        b_norm(j + 1)
                    if s == 1 and has(j - 3):
                        choose(j - 3)
                    if s == 2 and has(j - 2):
                        norm1(j - 2)
                    if s == 3 and has(j - 3):
                        place(j - 3)
                    lagged(norm_o, j, s, 2)
                    if s == 3 and has(j + 1):
                        copy_v(j + 1)

            dve.memset(w["bias_parts"][:, :], 0.0).then_inc(S["bias_chain"], 1)
            dve.wait_ge(S["bias_chain"], 1)
            dve.memset(cum[:, 0, :], 0.0)
            dve.memset(va[:, :, :, :, HD:HD + 1], 1.0)
            dve.memset(kz[:, 0, :, :, :], 0.0)
            dve.memset(kz[:, 1, :, :, :], 0.0).then_inc(S["kz_cleared"], 1)
            dve.wait_ge(S["kz_cleared"], 1)
            run_slots(slot, dve)

            chain = S["table_chain"]
            steps = [0]

            def link(i):
                steps[0] += 1
                i.then_inc(chain, 1)
                dve.wait_ge(chain, steps[0])

            dve.wait_ge(S["one_hot"], (GT + 2) * GROUPS)
            dve.wait_ge(S["ranks_counted"], GROUPS)
            dve.tensor_copy(cum_h[:, 0, :], cum[:, 0, :]).then_inc(S["cum_ready"], 1)
            link(dve.memset(onesr[:, :], 1.0))
            dve.wait_ge(S["counts_ready"], 1)
            link(dve.tensor_copy(cnt[:, :], ps_l[:, 0:EXPERTS]))
            link(dve.tensor_tensor(padf[:, 0:EXPERTS], cnt[:, :], shared["pad"][:, 0:EXPERTS], ALU.add))
            link(dve.tensor_copy(padf[:, EXPERTS:], shared["pad"][:, EXPERTS:EXPERTS + 1]))
            dve.tensor_copy(padi[:, :], padf[:, :]).then_inc(S["pad_indices"], 1)
            n128 = SEQS * LENGTH // P
            link(dve.tensor_tensor(more[:, :, :], cnt[:, :].unsqueeze(2).broadcast_to([P, EXPERTS, n128]),
                                   shared["multiples"][:, :].unsqueeze(1).broadcast_to([P, EXPERTS, n128]), ALU.is_gt))
            link(dve.tensor_reduce(tiles[:, :], more[:, :, :], AX.X, ALU.add))
            link(dve.tensor_tensor_scan(tend[:, :], onesr[:, :], tiles[:, :], 0.0, ALU.mult, ALU.add))
            index = shared["index"][:, :].unsqueeze(2).broadcast_to([P, TILES, EXPERTS])
            link(dve.tensor_tensor(full[:, :, :], tend[:, :].unsqueeze(1).broadcast_to([P, TILES, EXPERTS]), index,
                                   ALU.is_le))
            link(dve.tensor_reduce(te[:, :], full[:, :, :], AX.X, ALU.add))
            link(dve.tensor_tensor(part[:, :, :], full[:, :, :],
                                   tiles[:, :].unsqueeze(1).broadcast_to([P, TILES, EXPERTS]), ALU.mult))
            link(dve.tensor_reduce(tfirst[:, :], part[:, :, :], AX.X, ALU.add))
            link(dve.tensor_tensor(trow[:, :], shared["index"][:, :], tfirst[:, :], ALU.subtract))
            link(dve.tensor_scalar(live[:, :], te[:, :], float(EXPERTS), float(P), ALU.is_lt, ALU.mult))
            link(dve.tensor_tensor(trow[:, :], trow[:, :], live[:, :], ALU.mult))
            link(dve.scalar_tensor_tensor(out=trow[:, :], in0=te[:, :], scalar=float(CAP), in1=trow[:, :],
                                          op0=ALU.mult, op1=ALU.add))
            link(dve.tensor_copy(shared["tile_row"][:, :], trow[0:1, :]))
            link(dve.tensor_scalar(te[:, :], te[:, :], float(EXPERTS - 1), None, ALU.min))
            link(dve.tensor_copy(shared["tile_expert"][:, :], te[0:1, :]))

            bf, bparts, chain = w["biases"], w["bias_parts"], S["bias_chain"]
            dve.tensor_copy(bparts[0:EXPERTS, :], bf[:, :]).then_inc(chain, 1)
            dve.wait_ge(chain, 2)
            dve.tensor_tensor(bres[:, :], bf[:, :], bparts[0:EXPERTS, :], ALU.subtract).then_inc(chain, 1)
            dve.wait_ge(chain, 3)
            dve.tensor_copy(bmid[:, :], bres[:, :]).then_inc(chain, 1)
            dve.tensor_copy(bparts[32:32 + EXPERTS, :], bres[:, :]).then_inc(chain, 1)
            dve.wait_ge(chain, 5)
            dve.tensor_tensor(bparts[64:64 + EXPERTS, :], bres[:, :], bmid[:, :], ALU.subtract).then_inc(chain, 1)
            dve.wait_ge(chain, 6)

        @block.gpsimd
        def _(pool):
            pool.memset(mask_l[:, :], 0.0).then_inc(S["masks_cleared"], 1)
            pool.memset(mask_r[:, :, :], MASKED).then_inc(S["masks_cleared"], 1)
            pool.memset(before[:, :], 1.0).then_inc(S["masks_cleared"], 1)
            pool.memset(ones[:, :], 1.0).then_inc(S["masks_made"], 1)
            pool.wait_ge(S["masks_cleared"], 3)
            v = mask_l[:, :].rearrange("p (a l) -> p a l", l=POS)
            pool.affine_select(out=v, in_=v, compare_op=ALU.not_equal, fill=1.0, base=0,
                               pattern=[[0, P // POS], [-1, POS]], channel_multiplier=1).then_inc(S["masks_made"], 1)
            v = mask_r[:, :, :].rearrange("p h (a l) -> p (h a) l", l=POS)
            pool.affine_select(out=v, in_=v, compare_op=ALU.not_equal, fill=0.0, base=0,
                               pattern=[[0, HEADS * P // POS], [-1, POS]], channel_multiplier=1)\
                .then_inc(S["masks_made"], 1)
            pool.affine_select(out=before[:, :], in_=before[:, :], compare_op=ALU.is_gt, fill=0.0, base=0,
                               pattern=[[1, P]], channel_multiplier=-1).then_inc(S["masks_made"], 1)
            pool.memset(padrow[:, 0:2 * D], 0.0).then_inc(S["pad_row"], 1)
            pool.tensor_copy(padrow[:, 2 * D:].bitcast(I32), shared["ids"][:, GT * GROUPS:]).then_inc(S["pad_row"], 1)

            def root(out, var_eps, s_var, s_out, j):
                pool.wait_ge(s_var, j + 1)
                pool.tensor_tensor(out[:, :], var_eps[:, :], half_neg[:, :], ALU.pow).then_inc(s_out, 1)

            def row(i):
                return w["rows"][:, i, :].unsqueeze(1).broadcast_to([P, GT, D])

            def with_bias(j):
                pool.wait_ge(S["b_normed"], j + 1)
                if past(j, 2):
                    pool.wait_ge(S["r1_ready"], j - 1)
                pool.tensor_tensor(xb[:, parity(j), :, :], xn[:, parity(j), :, :], row(1), ALU.add)\
                    .then_inc(S["xb_ready"], 1)

            def scale_y(j):
                pool.wait_ge(S["r1_normed"], j + 1)
                if past(j, 1):
                    pool.wait_ge(S["y_ready"], j)
                pool.tensor_tensor(yg[:, :, :], yn[:, :, :], row(2), ALU.mult).then_inc(S["y_scaled"], 1)
                pool.wait_ge(S["y_scaled"], j + 1)
                if past(j, 2):
                    pool.wait_ge(S[f"rows_scattered{parity(j)}"], 8 * GT * (j - parity(j)))
                pool.tensor_tensor(pk[:, parity(j), :, 0:D], yg[:, :, :], row(3), ALU.add).then_inc(S["y_ready"], 1)

            def scatter(j):
                pool.wait_ge(S["dest_ready"], j + 1)
                pool.wait_ge(S[f"pk_x1_loaded{parity(j)}"], loads(j))
                pool.wait_ge(S["y_ready"], j + 1)
                pool.sem_inc(carrier, 1)
                for t in range(GT):
                    pool.indirect_dma_start(
                        out=routed[:, :], out_offset=bass.IndirectOffsetOnAxis(ap=desti[:, parity(j), t:t + 1], axis=0),
                        in_=pk[:, parity(j), t, :], in_offset=None).then_inc(S[f"rows_scattered{parity(j)}"], 16)

            def slot(j):
                if has(j + 1):
                    root(rstd, vare, S["b_variance"], S["b_rstd"], j + 1)
                if has(j - 2):
                    root(rstd1, vare1, S["r1_variance"], S["r1_rstd"], j - 2)
                if has(j):
                    with_bias(j)
                if has(j - 2):
                    scale_y(j - 2)
                if has(j - 3):
                    scatter(j - 3)

            run_slots(slot, pool)
            pool.wait_ge(S["pad_indices"], 1)
            pool.wait_ge(S["pad_row"], 2)
            for e in range(EXPERTS + 1):
                pool.indirect_dma_start(
                    out=routed[:, :], out_offset=bass.IndirectOffsetOnAxis(ap=padi[:, e:e + 1], axis=0),
                    in_=padrow[:, :], in_offset=None).then_inc(S["pad_scattered"], 16)
            pool.wait_ge(S["pad_scattered"], 16 * (EXPERTS + 1))
            for i in range(2):
                pool.wait_ge(S[f"rows_scattered{i}"], 8 * GT * GROUPS)


def experts(nc, sem, banks, sel, ident, half_neg, w, shared, carrier, routed, out):
    ctx = ExitStack()
    SLOTS = 4

    def sb(name, shape, dt=F32):
        return ctx.enter_context(nc.sbuf_tensor(name, shape, dt))

    with ctx:
        ps_yt, ps_h, ps_t, ps_f = banks[0:2], banks[2:4], banks[4:6], banks[6:8]

        rows = sb("rows", [P, SLOTS, 4, ROW])
        yT = sb("d_yT", [P, 2, P])
        hid = sb("hid", [P, 2, DF])
        hT = sb("hT", [P, 2, DF // P, P])
        bparts = w["bias_parts"]
        z0 = sb("z0", [P, 4, D])
        z1 = sb("z1", [P, 4, D])
        z2 = sb("z2", [P, 4, D])
        z3 = sb("z3", [P, 4, D])
        z4 = sb("z4", [P, 4, D])
        res = sb("res", [P, 2, 4, D])
        tokens = sb("tokens", [P, 2, 4], I32)
        stat = [sb(f"d_stat{i}", [P, 4, 6]) for i in range(2)]
        mv = [sb(f"d_mv{i}", [P, 4, 2]) for i in range(2)]
        vare = [sb(f"d_vare{i}", [P, 4]) for i in range(2)]
        rstd = [sb(f"d_rstd{i}", [P, 4]) for i in range(2)]

        names = """rows_loaded0 rows_loaded1 rows_loaded2 rows_loaded3 y_transposed yT_copied hidden_summed
            hidden_ready hidden_transposed hT_copied expert_summed z0_ready stats0 stats1 variance0 variance1
            rstd0 rstd1 z1_ready z2_ready z3_ready z4_ready res_ready
            out_scattered0 out_scattered1"""
        S = {n: sem("D_" + n) for n in names.split()}

        def fixed(q, n):
            if isinstance(q, int):
                return q % n
            assert q.out_of_modulus % n == 0
            return q.guaranteed_mod_val % n

        def past(q, n):
            if isinstance(q, int):
                return q >= n
            assert q.min_val >= n, "peel more quads"
            return True

        def run_slots(slot, engine):
            for q in range(SLOTS):
                slot(q)
            with engine.Fori(1, QUADS // SLOTS) as turn:
                for i in range(SLOTS):
                    slot(turn * SLOTS + i)
            for q in range(QUADS // SLOTS * SLOTS, QUADS + 2):
                slot(q)

        def lagged(q, i, lag):
            q, i = (q, i - lag) if i >= lag else (q - 1, i - lag + 4)
            if isinstance(q, int) and not 0 <= q < QUADS:
                return None
            return q, i

        block = ctx.enter_context(nc.Block())

        @block.sync
        def _(sp):
            def load(q):
                if past(q, SLOTS):
                    sp.wait_ge(S["res_ready"], 2 * (q - SLOTS + 1))
                    sp.sem_inc(carrier, 1)
                for i in range(4):
                    first = sp.value_load(shared["tile_row"][0:1, bass.ds(q * 4 + i, 1)], min_val=0,
                                          max_val=EXPERTS * CAP)
                    sp.dma_start(rows[:, fixed(q, SLOTS), i, :], routed[bass.ds(first, P), :])\
                      .then_inc(S[f"rows_loaded{fixed(q, SLOTS)}"], 16)

            def slot(q):
                if not isinstance(q, int) or q + 1 < QUADS:
                    load(q + 1)

            load(0)
            run_slots(slot, sp)
            for s in range(2):
                sp.wait_ge(S[f"out_scattered{s}"], 32 * QUADS)

        @block.tensor
        def _(pe):
            def turn_y(q, i):
                tile = q * 4 + i
                if i == 0:
                    s = fixed(q, SLOTS)
                    pe.wait_ge(S[f"rows_loaded{s}"], (q - s) // SLOTS * 64 + 64)
                if not isinstance(q, int) or tile >= 2:
                    pe.wait_ge(S["yT_copied"], tile - 1)
                pe.transpose(ps_yt[i % 2][:, 0:P], rows[:, fixed(q, SLOTS), i, 0:D], ident[:, :])\
                  .then_inc(S["y_transposed"], 1)

            def expert_of(tile):
                return pe.value_load(shared["tile_expert"][0:1, bass.ds(tile, 1)], min_val=0, max_val=EXPERTS - 1)

            def hidden(q, i):
                tile = q * 4 + i
                e = expert_of(tile)
                if not isinstance(q, int) or tile >= 2:
                    pe.wait_ge(S["hidden_ready"], tile - 1)
                pe.matmul(ps_h[i % 2][:, :], sel[:, bass.ds(e, 1), :].rearrange("p o m -> p (o m)"), bparts[:, 0:DF],
                          start=True, stop=False)
                pe.wait_ge(S["yT_copied"], tile + 1)
                pe.matmul(ps_h[i % 2][:, :], yT[:, i % 2, :], w["w1"][:, bass.ds(e, 1), :].rearrange("p o f -> p (o f)"),
                          start=False, stop=True).then_inc(S["hidden_summed"], 1)

            def turn_h(q, i):
                tile = q * 4 + i
                pe.wait_ge(S["hidden_ready"], tile + 1)
                if not isinstance(q, int) or tile >= 2:
                    pe.wait_ge(S["hT_copied"], tile - 1)
                for k in range(DF // P):
                    mm = pe.transpose(ps_t[i % 2][:, k * P:(k + 1) * P], hid[:, i % 2, k * P:(k + 1) * P], ident[:, :])
                mm.then_inc(S["hidden_transposed"], 1)

            def outward(q, i):
                tile = q * 4 + i
                e = expert_of(tile)
                if i == 0 and past(q, 2):
                    pe.wait_ge(S["z0_ready"], q - 1)
                dst = ps_f[fixed(q, 2)][:, i * D:(i + 1) * D]
                pe.matmul(dst, sel[:, bass.ds(e, 1), :].rearrange("p o m -> p (o m)"), bparts[:, DF:], start=True,
                          stop=False)
                pe.wait_ge(S["hT_copied"], tile + 1)
                for k in range(DF // P):
                    mm = pe.matmul(dst, hT[:, i % 2, k, :],
                                   w["w2"][:, bass.ds(e, 1), k, :].rearrange("p o d -> p (o d)"),
                                   start=False, stop=k == DF // P - 1)
                mm.then_inc(S["expert_summed"], 1)

            def slot(q):
                for i in range(4):
                    for lag, part in enumerate((turn_y, hidden, turn_h, outward)):
                        at = lagged(q, i, lag)
                        if at:
                            part(*at)

            run_slots(slot, pe)

        @block.scalar
        def _(act):
            def copy_yT(q, i):
                tile = q * 4 + i
                act.wait_ge(S["y_transposed"], tile + 1)
                if not isinstance(q, int) or tile >= 2:
                    act.wait_ge(S["hidden_summed"], tile - 1)
                act.activation(yT[:, i % 2, :], ps_yt[i % 2][:, 0:P], ACT.Copy).then_inc(S["yT_copied"], 1)

            def relu(q, i):
                tile = q * 4 + i
                act.wait_ge(S["hidden_summed"], tile + 1)
                if not isinstance(q, int) or tile >= 2:
                    act.wait_ge(S["hidden_transposed"], tile - 1)
                act.activation(hid[:, i % 2, :], ps_h[i % 2][:, :], ACT.Relu).then_inc(S["hidden_ready"], 1)

            def copy_hT(q, i):
                tile = q * 4 + i
                act.wait_ge(S["hidden_transposed"], tile + 1)
                if not isinstance(q, int) or tile >= 2:
                    act.wait_ge(S["expert_summed"], tile - 1)
                act.activation(hT[:, i % 2, :, :], ps_t[i % 2][:, :].rearrange("p (k t) -> p k t", t=P), ACT.Copy)\
                   .then_inc(S["hT_copied"], 1)

            def slot(q):
                for i in range(4):
                    for lag, part in ((0, copy_yT), (1, relu), (2, copy_hT)):
                        at = lagged(q, i, lag)
                        if at:
                            part(*at)

            run_slots(slot, act)

        @block.vector
        def _(dve):
            def stats(src, n, q):
                s_bn = S[f"stats{n}"]
                for t in range(4):
                    i = dve.bn_stats(stat[n][:, t, :], src[:, t, :])
                i.then_inc(s_bn, 1)
                dve.wait_ge(s_bn, 2 * q + 1)
                dve.sem_inc(carrier, 1)
                for t in range(4):
                    i = dve.bn_aggr(mv[n][:, t, :], stat[n][:, t, :])
                i.then_inc(s_bn, 1)
                dve.wait_ge(s_bn, 2 * q + 2)
                dve.tensor_scalar(vare[n][:, :], mv[n][:, :, 1], EPS, None, ALU.add).then_inc(S[f"variance{n}"], 1)

            def norm(dst, src, n, q, done):
                dve.wait_ge(S[f"rstd{n}"], q + 1)
                for t in range(4):
                    i = dve.tensor_scalar(dst[:, t, :], src[:, t, :], mv[n][:, t, 0:1], rstd[n][:, t:t + 1],
                                          ALU.subtract, ALU.mult)
                i.then_inc(S[done], 1)

            def add_y(q):
                dve.wait_ge(S["expert_summed"], 4 * (q + 1))
                if past(q, 1):
                    dve.wait_ge(S["z1_ready"], q)
                dve.tensor_tensor(z0[:, :, :], ps_f[fixed(q, 2)][:, :].rearrange("p (t d) -> p t d", t=4),
                                  rows[:, fixed(q, SLOTS), :, 0:D], ALU.add).then_inc(S["z0_ready"], 1)
                dve.wait_ge(S["z0_ready"], q + 1)
                stats(z0, 0, q)

            def norm2(q):
                if past(q, 1):
                    dve.wait_ge(S["z2_ready"], q)
                norm(z1, z0, 0, q, "z1_ready")

            def row(i):
                return w["rows"][:, i, :].unsqueeze(1).broadcast_to([P, 4, D])

            def affine(q):
                dve.wait_ge(S["z1_ready"], q + 1)
                if past(q, 1):
                    dve.wait_ge(S["z3_ready"], q)
                dve.tensor_tensor(z2[:, :, :], z1[:, :, :], row(4), ALU.mult).then_inc(S["z2_ready"], 1)
                dve.wait_ge(S["z2_ready"], q + 1)
                if past(q, 1):
                    dve.wait_ge(S["z4_ready"], q)
                dve.tensor_tensor(z3[:, :, :], z2[:, :, :], row(5), ALU.add).then_inc(S["z3_ready"], 1)

            def stats2(q):
                dve.wait_ge(S["z3_ready"], q + 1)
                stats(z3, 1, q)

            def norm3(q):
                if past(q, 1):
                    dve.wait_ge(S["res_ready"], 2 * q)
                norm(z4, z3, 1, q, "z4_ready")

            def quad(q):
                return not isinstance(q, int) or 0 <= q < QUADS

            def slot(q):
                for i in range(4):
                    if i == 0 and quad(q - 2):
                        norm2(q - 2)
                        affine(q - 2)
                    if i == 1 and quad(q - 2):
                        stats2(q - 2)
                    if i == 3 and quad(q - 1):
                        add_y(q - 1)
                    if i == 3 and quad(q - 2):
                        norm3(q - 2)

            run_slots(slot, dve)

        @block.gpsimd
        def _(pool):
            def root(n, q):
                pool.wait_ge(S[f"variance{n}"], q + 1)
                pool.tensor_tensor(rstd[n][:, :], vare[n][:, :], half_neg[:, :], ALU.pow).then_inc(S[f"rstd{n}"], 1)

            def add_x1(q):
                par = fixed(q, SLOTS)
                pool.wait_ge(S["z4_ready"], q + 1)
                if past(q, 2):
                    s = fixed(q, 2)
                    pool.wait_ge(S[f"out_scattered{s}"], 32 * (q - s))
                pool.tensor_tensor(res[:, fixed(q, 2), :, :], z4[:, :, :], rows[:, par, :, D:2 * D], ALU.add)\
                    .then_inc(S["res_ready"], 1)
                pool.tensor_copy(tokens[:, fixed(q, 2), :], rows[:, par, :, 2 * D].bitcast(I32))\
                    .then_inc(S["res_ready"], 1)

            def scatter(q):
                pool.wait_ge(S["res_ready"], 2 * q + 2)
                pool.sem_inc(carrier, 1)
                for i in range(4):
                    pool.indirect_dma_start(
                        out=out[:, :],
                        out_offset=bass.IndirectOffsetOnAxis(ap=tokens[:, fixed(q, 2), i:i + 1], axis=0),
                        in_=res[:, fixed(q, 2), i, :], in_offset=None, bounds_check=SEQS * LENGTH - 1,
                        oob_is_err=False).then_inc(S[f"out_scattered{fixed(q, 2)}"], 16)

            def quad(q):
                return not isinstance(q, int) or 0 <= q < QUADS

            def slot(q):
                if quad(q - 2):
                    root(1, q - 2)
                if quad(q - 1):
                    root(0, q - 1)
                if quad(q - 2):
                    add_x1(q - 2)
                    scatter(q - 2)

            run_slots(slot, pool)


def build(nc, x, w_in_t, per_channel, w_x_t, w_dt_t, w_out_t, wqkv_t, bqk, wo_t, wg_t, rows, biases, w1, w2,
          consts, ids, out):
    x1 = nc.dram_tensor("x1_rows", [SEQS * LENGTH, D], F32, kind="Internal").ap()
    routed = nc.dram_tensor("routed", [EXPERTS * CAP + P, ROW], F32, kind="Internal").ap()
    with ExitStack() as ctx:
        def sb(name, shape, dt=F32):
            return ctx.enter_context(nc.sbuf_tensor(name, shape, dt))

        def sem(name):
            return ctx.enter_context(nc.semaphore(name))

        banks = [ctx.enter_context(nc.psum_tensor(f"bank{i}", [P, 512], F32)) for i in range(8)]
        sel = sb("sel", [96, 2 * NST, P], BF16)
        ident = sb("ident", [P, P])
        half_neg = sb("half_neg", [P, 4])
        w = {"wqk": sb("w_qkv", [P, 3 * D]), "bqk": sb("b_qk", [P, 2]), "wo": sb("w_o", [P, D]),
             "wg": sb("w_g", [P, EXPERTS]), "rows": sb("row_params", [P, 6, D]),
             "w1": sb("w_1", [P, EXPERTS, DF]), "w2": sb("w_2", [P, EXPERTS, DF // P, D]),
             "biases": sb("biases", [EXPERTS, DF + D]), "bias_parts": sb("bias_parts", [96, DF + D], BF16)}
        table = sb("table", [P, consts.shape[1]])
        idt = sb("idt", [P, ids.shape[1]], I32)
        at, shared = 0, {"ids": idt, "tile_row": sb("tile_row", [1, TILES], I32),
                         "tile_expert": sb("tile_expert", [1, TILES], I32)}
        for name, n in TABLE:
            shared[name] = table[:, at:at + n]
            at += n
        late = [(w["wqk"][:, :], wqkv_t), (w["bqk"][:, :], bqk), (w["wo"][:, :], wo_t), (w["wg"][:, :], wg_t),
                (w["rows"][:, :, :].rearrange("p i d -> p (i d)"), rows.partition_broadcast(P)),
                (table[:, :], consts), (idt[:, :], ids), (w["biases"][:, :], biases),
                (w["w1"][:, :, :], w1.rearrange("e p f -> p e f")),
                (w["w2"][:, :, :, :], w2.rearrange("e (k p) d -> p e k d", p=P))]
        carrier = sem("waits_carried")
        s_late = sem("late_weights_loaded")
        mamba(nc, sem, carrier, banks, sel, ident, half_neg, x, w_in_t, per_channel, w_x_t, w_dt_t, w_out_t, x1, late, s_late)
        attention(nc, sem, carrier, banks, ident, half_neg, w, shared, x1, routed)
        experts(nc, sem, banks, sel, ident, half_neg, w, shared, carrier, routed, out)


TABLE = (("order", EXPERTS), ("region", EXPERTS), ("pad", EXPERTS + 1), ("multiples", SEQS * LENGTH // P),
         ("index", TILES))


def kernel(**inputs):
    import numpy as np
    import concourse.bacc as bacc
    from concourse.bass_utils import run_bass_kernel_spmd

    a = {k: np.asarray(v) for k, v in inputs.items()}

    def lay(v):
        return np.ascontiguousarray(v)

    def blocks(name):
        return a[name].reshape(CH, P, -1).transpose(1, 0, 2).reshape(P, -1)

    p = np.arange(P)
    cols = {"order": np.tile(EXPERTS - np.arange(EXPERTS), (P, 1)),
            "region": np.tile(CAP * np.arange(EXPERTS), (P, 1)),
            "pad": p[:, None] + CAP * np.arange(EXPERTS + 1)[None, :],
            "multiples": np.tile(P * np.arange(SEQS * LENGTH // P), (P, 1)),
            "index": np.tile(np.arange(TILES), (P, 1))}
    consts = np.concatenate([cols[name] for name, _ in TABLE], 1).astype(np.float32)
    tile, half = np.divmod(np.arange(GROUPS * GT), 2)
    ids = (p[:, None] // POS) * LENGTH + p[:, None] % POS + half[None, :] * HALF + tile[None, :] * POS
    ids = np.concatenate([ids, np.full((P, 1), 1 << 20)], 1).astype(np.int32)

    arrays = {
        "x": a["L0_attn_x"].reshape(SEQS, 2, HALF, D).transpose(1, 0, 2, 3).reshape(-1, D),
        "w_in_t": a["L0_attn_W_in"].T,
        "per_channel": np.concatenate([blocks("L0_attn_" + n) for n in ("conv_w", "conv_b", "b_dt", "Dp", "A_log")], 1),
        "w_x_t": a["L0_attn_W_x"].T,
        "w_dt_t": a["L0_attn_W_dt"].T,
        "w_out_t": a["L0_attn_W_out"].T,
        "wqkv_t": a["L0_ffn_Wqkv"].T,
        "bqk": a["L0_ffn_bqkv"][0:2 * D].reshape(2, D).T,
        "wo_t": a["L0_ffn_Wo"].T,
        "wg_t": a["L0_ffn_Wg"].T,
        "rows": np.concatenate([a["L0_ffn_bqkv"][2 * D:]] + [a["L0_ffn_" + n] for n in ("bo", "g1", "be1", "g2", "be2")]),
        "biases": np.concatenate([a["L0_ffn_b1"], a["L0_ffn_b2"]], 1),
        "w1": a["L0_ffn_W1"],
        "w2": a["L0_ffn_W2"],
        "consts": consts,
        "ids": ids,
    }
    nc = bacc.Bacc("TRN2", target_bir_lowering=False, num_devices=1)
    arrays = {"in_" + k: lay(v) for k, v in arrays.items()}
    args = [nc.dram_tensor(k, v.shape, mybir.dt.from_np(v.dtype), kind="ExternalInput").ap() for k, v in arrays.items()]
    out = nc.dram_tensor("out", [SEQS * LENGTH, D], F32, kind="ExternalOutput").ap()
    build(nc, *args, out)
    r = run_bass_kernel_spmd(nc, [arrays], core_ids=[0])
    return r.results[0]["out"].reshape(SEQS, LENGTH, D)
```

```python
from contextlib import ExitStack

import concourse.bass as bass
from concourse import mybir

ALU = mybir.AluOpType
ACT = mybir.ActivationFunctionType
AX = mybir.AxisListType
F32 = mybir.dt.float32
BF16 = mybir.dt.bfloat16
I32 = mybir.dt.int32
P = 128

SEQS, LENGTH, D = 8, 1024, 128
DI, NST, RANK, TAPS = 256, 16, 64, 4
HEADS, HD, EXPERTS, DF = 4, 32, 8, 512
EPS = 1e-5
HALF = 512
STEPS = SEQS * LENGTH // HALF
CH = DI // P
TT = HALF // P
RING = 4
AT = {"stats": 0, "root": 0, "norm": 1, "carry_in": 1, "transpose": 2, "xnT": 2, "xcp0": 2, "xc0": 3,
      "skip": 3, "xc1": 4, "xcp1": 4, "gate": 4, "z0": 5, "tap0_0": 5, "tap0_1": 5, "z1": 6, "tap1": 6,
      "tap2": 6, "tap3": 8, "carry_out": 8, "silu": 8, "split": 9, "dbc": 10, "res": 10, "mid": 10,
      "dt0": 10, "softplus0": 10, "dt1": 11, "softplus1": 11, "softlog": 11, "lo": 13, "delta": 13,
      "u": 13, "project": 13, "out_stats": 14, "out_root": 14, "out_norm": 14, "add": 15}
LN_SET = "natural_log_exp_and_others"


def mamba(nc, sem, carrier, banks, sel, ident, half_neg, x, w_in_t, per_channel, w_x_t, w_dt_t, w_out_t, x1,
          late_loads, s_late):
    ctx = ExitStack()

    def sb(name, shape, dt=F32):
        return ctx.enter_context(nc.sbuf_tensor(name, shape, dt))

    with ctx:
        ps_y, ps_b, ps_c = banks[0:2], banks[2:4], banks[4:6]
        m0, m1 = banks[6:8]

        w_in = sb("w_in", [P, 2 * DI])
        chan = sb("chan", [P, CH * (TAPS + 3 + NST)])
        cw = chan[:, 0:CH * TAPS].rearrange("p (c k) -> p c k", c=CH)
        cb, bdt, dpw = (chan[:, CH * (TAPS + i):CH * (TAPS + i + 1)] for i in range(3))
        alog = chan[:, CH * (TAPS + 3):].rearrange("p (c n) -> p c n", c=CH)
        w_x = sb("w_x", [P, CH, P])
        w_dt = sb("w_dt", [P, DI])
        aneg = sb("aneg", [P, CH, NST])
        w_out = sb("w_out", [P, CH, D])

        xin = sb("xin", [P, TT, D])
        stat = sb("stat", [P, TT, 6])
        mv = sb("mv", [P, TT, 2])
        vare = sb("vare", [P, TT])
        rstd = sb("rstd", [P, TT])
        nmean = sb("nmean", [P, TT])
        shift = sb("shift", [P, TT])
        xn = sb("xn", [P, TT, D])
        xnT = sb("xnT", [P, HALF])
        xcp = sb("xcp", [P, CH, TAPS - 1 + HALF])
        cacc = sb("cacc", [P, CH, HALF])
        dlow = sb("dlow", [P, HALF])
        res1 = sb("res1", [32, HALF])
        mid0 = sb("mid0", [32, HALF], BF16)
        sp_abs = sb("sp_abs", [P, CH, HALF])
        sp_relu = sb("sp_relu", [P, CH, HALF])
        xc = sb("xc", [P, 2, CH, HALF])
        zs = sb("zs", [P, 2, CH, HALF])
        delta = sb("delta", [P, 2, CH, HALF])
        u = sb("u", [P, 2, CH, HALF])
        bcs = sb("bcs", [96, 2, HALF], BF16)
        hstate = sb("hstate", [P, (STEPS + SEQS) * NST * CH])
        ccarry = sb("ccarry", [P, STEPS + SEQS, CH, TAPS - 1])
        abuf = sb("abuf", [P, RING, CH, HALF])
        bx = sb("bx", [P, 2, CH, HALF])
        hbuf = sb("hbuf", [P, RING, CH, HALF])
        crep = sb("crep", [P, RING, HALF])
        cm = sb("cm", [P, RING, CH, HALF])
        xres = sb("xres", [P, TT, D])
        yd = sb("yd", [P, CH, HALF])
        yg = sb("yg", [P, CH, HALF])
        tstat = sb("tstat", [P, TT, 6])
        tmv = sb("tmv", [P, TT, 2])
        tvare = sb("tvare", [P, TT])
        trstd = sb("trstd", [P, TT])
        tnmean = sb("tnmean", [P, TT])
        tshift = sb("tshift", [P, TT])
        on = sb("on", [P, TT, D])
        x1t = sb("x1t", [P, TT, D])

        s_w = sem("weights_loaded")
        s_ident = sem("ident_made")
        s_sel = sem("sel_made")
        s_sel0 = sem("sel_cleared")
        s_consts = sem("constants_set")
        s_aexp = sem("a_exponentiated")
        s_aneg = sem("a_negated")
        s_xin = sem("xin_loaded")
        s_fstat = sem("front_stats")
        s_fvar = sem("front_variance")
        s_frstd = sem("front_rstd")
        s_xn = sem("xn_normed")
        s_tp = sem("xn_transposed")
        s_xnT = sem("xnT_copied")
        s_xcp_mm = sem("xc_projected")
        s_z_mm = sem("z_projected")
        s_xcp = sem("xcp_copied")
        s_cc = sem("carry_copied")
        s_tap0 = sem("tap0_done")
        s_tap = sem("taps_done")
        s_silu = sem("silu_done")
        s_dbc = sem("dbc_projected")
        s_hi = sem("bc_hi_split")
        s_dlow = sem("dlow_copied")
        s_res = sem("bc_residual")
        s_mid = sem("bc_mid_split")
        s_bcs = sem("bc_split")
        s_dt = sem("dt_projected")
        s_sp = sem("softplus_parts")
        s_spln = sem("softplus_log")
        s_delta = sem("delta_ready")
        s_u = sem("u_ready")
        s_brep = sem("b_spread")
        s_crep = sem("c_spread")
        s_a = sem("decay_ready")
        s_cs = sem("c_copied")
        s_bx = sem("bx_ready")
        s_scan = sem("scan_done")
        s_save = sem("state_saved")
        s_cm = sem("cm_ready")
        s_y = sem("y_summed")
        s_yd = sem("yd_ready")
        s_yg = sem("yg_ready")
        s_om = sem("out_projected")
        s_tstat = sem("tail_stats")
        s_tvar = sem("tail_variance")
        s_trstd = sem("tail_rstd")
        s_on = sem("out_normed")
        s_xres = sem("xres_loaded")
        s_x1 = sem("x1_ready")
        s_x1st = sem("x1_stored")

        block = ctx.enter_context(nc.Block())
        NW = 6

        x_t = x.rearrange("(g t p) d -> g p t d", t=TT, p=P)
        x1_t = x1.rearrange("(t a g l) d -> g t a l d", t=TT, a=P // 16, g=STEPS)

        def parity(g):
            return (g if isinstance(g, int) else g.guaranteed_mod_val) % 2

        def run_steps(part, engine):
            part(0, True, False)
            with engine.Fori(0, (STEPS - 2) // 2) as pair:
                part(pair * 2 + 1, False, False)
                part(pair * 2 + 2, False, False)
            part(STEPS - 1, False, True)

        @block.sync
        def _(sp):
            for dst, src in ((w_in[:, :], w_in_t),
                             (w_x[:, :, 0:32], w_x_t[:, RANK:RANK + 32].rearrange("(c p) r -> p c r", p=P)),
                             (w_x[:, :, 64:128], w_x_t[:, 0:RANK].rearrange("(c p) r -> p c r", p=P)),
                             (w_dt[64:128, :], w_dt_t),
                             (chan[:, :], per_channel),
                             (w_out[:, :, :], w_out_t.rearrange("(c p) d -> p c d", p=P))):
                sp.dma_start(dst, src).then_inc(s_w, 16)

            def load_x(f):
                sp.dma_start(xin[:, :, :], x_t[bass.ds(f, 1)].rearrange("o p t d -> (o p) t d")).then_inc(s_xin, 16)

            def store_x1(t):
                for j in range(TT):
                    sp.dma_start(x1_t[bass.ds(t, 1), j].rearrange("o a l d -> (o a) l d"),
                                 x1t[:, j, :]).then_inc(s_x1st, 16)

            def step(g):
                if not isinstance(g, int) or g + 2 < STEPS:
                    sp.wait_ge(s_xn, g + 2)
                    load_x(g + 2)
                if isinstance(g, int) and g == 0:
                    for dst, src in late_loads:
                        sp.dma_start(dst, src).then_inc(s_late, 16)
                else:
                    sp.wait_ge(s_x1, g)
                    store_x1(g - 1)
                sp.dma_start(xres[:, :, :], x_t[bass.ds(g, 1)].rearrange("o p t d -> (o p) t d")).then_inc(s_xres, 16)

            load_x(0)
            sp.wait_ge(s_xn, 1)
            load_x(1)
            step(0)
            with sp.Fori(1, STEPS - 2) as g:
                step(g)
            step(STEPS - 2)
            step(STEPS - 1)
            sp.wait_ge(s_x1, STEPS)
            store_x1(STEPS - 1)
            sp.wait_ge(s_x1st, 16 * TT * STEPS)
            sp.wait_ge(s_late, 16 * len(late_loads))

        @block.tensor
        def _(pe):
            def f_transpose(f):
                pe.wait_ge(s_xn, f + 1)
                if not isinstance(f, int) or f >= 1:
                    pe.wait_ge(s_sp, 2 * f)
                for t in range(TT):
                    mm = pe.transpose(m1[:, t * P:(t + 1) * P], xn[:, t, :], ident[:, :])
                mm.then_inc(s_tp, 1)

            def f_xc(f, c):
                if c == 0:
                    pe.wait_ge(s_xnT, f + 1)
                else:
                    pe.wait_ge(s_xcp, 2 * f + 1)
                pe.matmul(m1[:, :], w_in[:, c * P:(c + 1) * P], xnT[:, :],
                          start=True, stop=True).then_inc(s_xcp_mm, 1)

            def f_z(f, c):
                if c == 0:
                    pe.wait_ge(s_xcp, 2 * f + 2)
                elif not isinstance(f, int) or f >= 1:
                    pe.wait_ge(s_sp, 2 * f)
                    if not isinstance(f, int) or f >= 3:
                        pe.wait_ge(s_on, f - 2)
                pe.matmul((m1, m0)[c][:, :], w_in[:, DI + c * P:DI + (c + 1) * P], xnT[:, :],
                          start=True, stop=True).then_inc(s_z_mm, 1)

            def f_dbc(f):
                pe.wait_ge(s_silu, 4 * f + 4)
                for c in range(CH):
                    mm = pe.matmul(m1[:, :], w_x[:, c, :], xc[:, parity(f), c, :], start=c == 0, stop=c == CH - 1)
                mm.then_inc(s_dbc, 1)

            def f_dt(f, c):
                pe.wait_ge(s_dlow, f + 1)
                if c == 1:
                    pe.wait_ge(s_res, f + 1)
                pe.matmul((m0, m1)[c][:, :], w_dt[64:128, c * P:(c + 1) * P], dlow[64:128, :],
                          start=True, stop=True).then_inc(s_dt, 1)

            def spread(g, n):
                k = g * NST + n
                early = isinstance(g, int) and k < 2
                if n == 0:
                    pe.wait_ge(s_bcs, g + 1)
                if not early:
                    pe.wait_ge(s_bx, k - 1)
                rhs = bcs[:, parity(g), :]
                pe.matmul(ps_b[n % 2][:, :], sel[:, n, :], rhs, start=True, stop=True).then_inc(s_brep, 1)
                if not early:
                    pe.wait_ge(s_cs, k - 1)
                pe.matmul(ps_c[n % 2][:, :], sel[:, NST + n, :], rhs, start=True, stop=True).then_inc(s_crep, 1)

            def sum_state(g, n):
                pe.wait_ge(s_cm, g * NST + n + 1)
                if n == 0 and not (isinstance(g, int) and g == 0):
                    pe.wait_ge(s_yd, 2 * g)
                for c in range(CH):
                    mm = pe.matmul(ps_y[c][:, :], ident[:, :], cm[:, n % RING, c, :],
                                   start=n == 0, stop=n == NST - 1)
                mm.then_inc(s_y, 1)

            def t_project(t):
                pe.wait_ge(s_yg, t + 1)
                if isinstance(t, int) and t >= STEPS - 2:
                    pe.wait_ge(s_on, t)
                else:
                    pe.wait_ge(s_sp, 2 * t + 5)
                for j in range(TT):
                    for c in range(CH):
                        mm = pe.matmul(m0[:, j * P:(j + 1) * P], yg[:, c, j * P:(j + 1) * P], w_out[:, c, :],
                                       start=c == 0, stop=c == CH - 1)
                mm.then_inc(s_om, 1)

            def front_at(f, n):
                for at, part in (("transpose", lambda: f_transpose(f)), ("xc0", lambda: f_xc(f, 0)),
                                 ("xc1", lambda: f_xc(f, 1)), ("z0", lambda: f_z(f, 0)), ("z1", lambda: f_z(f, 1)),
                                 ("dbc", lambda: f_dbc(f)), ("dt0", lambda: f_dt(f, 0)), ("dt1", lambda: f_dt(f, 1))):
                    if n == AT[at]:
                        part()

            def step(g, first, last):
                for n in range(NST):
                    if n < NST - 1:
                        spread(g, n + 1)
                    elif not last:
                        spread(g + 1, 0)
                    if not last:
                        front_at(g + 1, n)
                    if n >= 3:
                        sum_state(g, n - 3)
                    elif not first:
                        sum_state(g - 1, NST - 3 + n)
                    if n == AT["project"] and not first:
                        t_project(g - 1)

            pe.wait_ge(s_w, 16 * NW)
            pe.wait_ge(s_ident, 1)
            for n in range(NST):
                front_at(0, n)
            pe.wait_ge(s_sel, 1)
            spread(0, 0)
            run_steps(step, pe)
            for n in range(NST - 3, NST):
                sum_state(STEPS - 1, n)
            t_project(STEPS - 1)

        @block.scalar
        def _(act):
            def f_norm(f):
                act.wait_ge(s_frstd, 2 * f + 2)
                if not isinstance(f, int) or f >= 1:
                    act.wait_ge(s_tp, f)
                for t in range(TT):
                    i = act.activation(xn[:, t, :], xin[:, t, :], ACT.Identity, bias=shift[:, t:t + 1],
                                       scale=rstd[:, t:t + 1])
                i.then_inc(s_xn, 1)

            def t_norm(t):
                act.wait_ge(s_trstd, 2 * t + 2)
                if not isinstance(t, int) or t >= 1:
                    act.wait_ge(s_x1, t)
                for j in range(TT):
                    i = act.activation(on[:, j, :], m0[:, j * P:(j + 1) * P], ACT.Identity, bias=tshift[:, j:j + 1],
                                       scale=trstd[:, j:j + 1])
                i.then_inc(s_on, 1)

            def f_xnT(f):
                act.wait_ge(s_tp, f + 1)
                if not isinstance(f, int) or f >= 1:
                    act.wait_ge(s_z_mm, 2 * f)
                act.activation(xnT[:, :], m1[:, :], ACT.Copy).then_inc(s_xnT, 1)

            def f_xcp(f, c):
                act.wait_ge(s_xcp_mm, 2 * f + 1 + c)
                if not isinstance(f, int) or f >= 1:
                    act.wait_ge(s_tap, 6 * f)
                    act.wait_ge(s_cc, 2 * f)
                act.activation(xcp[:, c, TAPS - 1:], m1[:, :], ACT.Copy).then_inc(s_xcp, 1)

            def f_tap0(f, c):
                act.wait_ge(s_xcp, 2 * f + 1 + c)
                act.wait_ge(s_cc, 2 * f + 1)
                if not isinstance(f, int) or f >= 1:
                    act.wait_ge(s_silu, 4 * f)
                act.activation(cacc[:, c, :], xcp[:, c, 0:HALF], ACT.Identity,
                               bias=cb[:, c:c + 1], scale=cw[:, c, 0:1]).then_inc(s_tap0, 1)

            def f_silu(f):
                act.wait_ge(s_z_mm, 2 * f + 2)
                if not isinstance(f, int) or f >= 2:
                    act.wait_ge(s_yg, f - 1)
                    act.wait_ge(s_u, f - 1)
                for c in range(CH):
                    act.activation(zs[:, parity(f), c, :], (m1, m0)[c][:, :], ACT.Silu).then_inc(s_silu, 1)
                for c in range(CH):
                    act.wait_ge(s_tap, 6 * f + 5 + c)
                    act.activation(xc[:, parity(f), c, :], cacc[:, c, :], ACT.Silu).then_inc(s_silu, 1)
                act.preload_act_table_set(LN_SET)

            def f_split(f):
                bcf = bcs[:, parity(f), :]
                act.wait_ge(s_dbc, f + 1)
                if not isinstance(f, int) or f >= 2:
                    act.wait_ge(s_crep, (f - 1) * NST)
                act.activation(bcf[0:32, :], m1[0:32, :], ACT.Copy).then_inc(s_hi, 1)
                if not isinstance(f, int) or f >= 1:
                    act.wait_ge(s_dt, 2 * f)
                act.activation(dlow[64:128, :], m1[64:128, :], ACT.Copy).then_inc(s_dlow, 1)

            def f_mid(f):
                bcf = bcs[:, parity(f), :]
                act.wait_ge(s_res, f + 1)
                if not isinstance(f, int) or f >= 1:
                    act.wait_ge(s_bcs, f)
                act.activation(mid0[:, :], res1[:, :], ACT.Copy).then_inc(s_mid, 1)
                act.activation(bcf[32:64, :], res1[:, :], ACT.Copy).then_inc(s_mid, 1)

            def f_softplus(f, c):
                act.wait_ge(s_dt, 2 * f + 1 + c)
                if not isinstance(f, int) or f >= 1:
                    act.wait_ge(s_delta, f)
                act.activation(sp_abs[:, c, :], (m0, m1)[c][:, :], ACT.Abs, bias=bdt[:, c:c + 1])
                act.activation(sp_relu[:, c, :], (m0, m1)[c][:, :], ACT.Relu, bias=bdt[:, c:c + 1]).then_inc(s_sp, 1)

            def f_softlog(f):
                act.wait_ge(s_sp, 2 * f + 2)
                act.activation(sp_abs[:, :, :], sp_abs[:, :, :], ACT.Exp, scale=-1.0).then_inc(s_spln, 1)
                act.wait_ge(s_spln, 2 * f + 1)
                act.activation(sp_abs[:, :, :], sp_abs[:, :, :], ACT.Ln, bias=1.0).then_inc(s_spln, 1)

            def decay(g, n):
                k = g * NST + n
                if n == 0:
                    act.wait_ge(s_delta, g + 1)
                if not (isinstance(g, int) and k < RING):
                    act.wait_ge(s_scan, 2 * (k - RING + 1))
                for c in range(CH):
                    e = act.activation(abuf[:, n % RING, c, :], delta[:, parity(g), c, :], ACT.Exp,
                                       scale=aneg[:, c, n:n + 1])
                e.then_inc(s_a, 1)

            def c_copy(g, n):
                k = g * NST + n
                act.wait_ge(s_crep, k + 1)
                if not (isinstance(g, int) and k < RING):
                    act.wait_ge(s_cm, k - RING + 1)
                act.activation(crep[:, n % RING, :], ps_c[n % 2][:, :], ACT.Copy).then_inc(s_cs, 1)

            def front_at(f, n):
                for at, part in (("norm", lambda: f_norm(f)), ("xnT", lambda: f_xnT(f)),
                                 ("xcp0", lambda: f_xcp(f, 0)), ("xcp1", lambda: f_xcp(f, 1)),
                                 ("tap0_0", lambda: f_tap0(f, 0)), ("tap0_1", lambda: f_tap0(f, 1)),
                                 ("silu", lambda: f_silu(f)), ("split", lambda: f_split(f)), ("mid", lambda: f_mid(f)),
                                 ("softplus0", lambda: f_softplus(f, 0)), ("softplus1", lambda: f_softplus(f, 1)),
                                 ("softlog", lambda: f_softlog(f))):
                    if n == AT[at]:
                        part()

            def step(g, first, last):
                for n in range(NST):
                    if n < NST - 1:
                        decay(g, n + 1)
                        c_copy(g, n + 1)
                    elif not last:
                        decay(g + 1, 0)
                        c_copy(g + 1, 0)
                    if not last:
                        front_at(g + 1, n)
                    if n == AT["out_norm"] and not first:
                        t_norm(g - 1)

            act.preload_act_table_set(LN_SET)
            act.wait_ge(s_w, 16 * NW)
            act.activation(aneg[:, :, :], alog, ACT.Exp).then_inc(s_aexp, 1)
            act.wait_ge(s_aexp, 1)
            act.activation(aneg[:, :, :], aneg[:, :, :], ACT.Copy, scale=-1.0).then_inc(s_aneg, 1)
            for n in range(NST):
                front_at(0, n)
            act.wait_ge(s_aneg, 1)
            decay(0, 0)
            c_copy(0, 0)
            run_steps(step, act)
            t_norm(STEPS - 1)

        @block.vector
        def _(dve):
            def norm_stats(src, st, mean_var, s_bn, s_var, var_eps, less_mean, count):
                for t in range(TT):
                    i = dve.bn_stats(st[:, t, :], src(t))
                i.then_inc(s_bn, 1)
                dve.wait_ge(s_bn, 2 * count + 1)
                dve.sem_inc(carrier, 1)
                dve.wait_ge(s_consts, 1)
                for t in range(TT):
                    i = dve.bn_aggr(mean_var[:, t, :], st[:, t, :])
                i.then_inc(s_bn, 1)
                dve.wait_ge(s_bn, 2 * count + 2)
                dve.tensor_scalar(var_eps[:, :], mean_var[:, :, 1], EPS, None, ALU.add)
                dve.tensor_scalar(less_mean[:, :], mean_var[:, :, 0], -1.0, None, ALU.mult).then_inc(s_var, 1)

            def f_stats(f):
                dve.wait_ge(s_xin, 16 * (f + 1))
                norm_stats(lambda t: xin[:, t, :], stat, mv, s_fstat, s_fvar, vare, nmean, f)

            def f_carry_in(f):
                if not isinstance(f, int) or f >= 1:
                    dve.wait_ge(s_tap0, 2 * f)
                    dve.wait_ge(s_tap, 6 * f)
                dve.wait_ge(s_cc, 2 * f)
                dve.tensor_copy(xcp[:, :, 0:TAPS - 1],
                                ccarry[:, bass.ds(f, 1), :, :].rearrange("p o c k -> p (o c) k")).then_inc(s_cc, 1)

            def f_carry_out(f):
                dve.wait_ge(s_xcp, 2 * f + 2)
                dve.tensor_copy(ccarry[:, bass.ds(f + SEQS, 1), :, :].rearrange("p o c k -> p (o c) k"),
                                xcp[:, :, HALF:]).then_inc(s_cc, 1)

            def f_tap(f, k):
                for c in range(CH):
                    if k == 1:
                        dve.wait_ge(s_tap0, 2 * f + 1 + c)
                    else:
                        dve.wait_ge(s_tap, 6 * f + 2 * (k - 2) + 1 + c)
                    dve.scalar_tensor_tensor(out=cacc[:, c, :], in0=xcp[:, c, k:k + HALF], scalar=cw[:, c, k:k + 1],
                                             in1=cacc[:, c, :], op0=ALU.mult, op1=ALU.add).then_inc(s_tap, 1)

            def f_res(f):
                bcf = bcs[:, parity(f), :]
                dve.wait_ge(s_hi, f + 1)
                if not isinstance(f, int) or f >= 1:
                    dve.wait_ge(s_mid, 2 * f)
                    dve.wait_ge(s_bcs, f)
                dve.tensor_tensor(res1[:, :], m1[0:32, :], bcf[0:32, :], ALU.subtract).then_inc(s_res, 1)

            def f_lo(f):
                bcf = bcs[:, parity(f), :]
                dve.wait_ge(s_mid, 2 * f + 2)
                dve.tensor_tensor(bcf[64:96, :], res1[:, :], mid0[:, :], ALU.subtract).then_inc(s_bcs, 1)

            def f_delta(f):
                dve.wait_ge(s_spln, 2 * f + 2)
                if not isinstance(f, int) or f >= 2:
                    dve.wait_ge(s_a, (f - 1) * NST)
                    dve.wait_ge(s_u, f - 1)
                dve.tensor_tensor(delta[:, parity(f), :, :], sp_abs[:, :, :], sp_relu[:, :, :], ALU.add).then_inc(s_delta, 1)

            def make_bx(g, n):
                k = g * NST + n
                if n == 0:
                    dve.wait_ge(s_u, g + 1)
                dve.wait_ge(s_brep, k + 1)
                if not (isinstance(g, int) and k < 2):
                    dve.wait_ge(s_scan, 2 * (k - 1))
                b = ps_b[n % 2][:, :].unsqueeze(1).broadcast_to([P, CH, HALF])
                dve.tensor_tensor(bx[:, n % 2, :, :], u[:, parity(g), :, :], b, ALU.mult).then_inc(s_bx, 1)

            def scan(g, n):
                k = g * NST + n
                dve.wait_ge(s_a, k + 1)
                dve.wait_ge(s_bx, k + 1)
                if not (isinstance(g, int) and k < RING):
                    dve.wait_ge(s_cm, k - RING + 1)
                    if n % RING == 0:
                        dve.wait_ge(s_save, g * (NST // RING) + n // RING)
                for c in range(CH):
                    dve.tensor_tensor_scan(hbuf[:, n % RING, c, :], abuf[:, n % RING, c, :], bx[:, n % 2, c, :],
                                           hstate[:, bass.ds(g * (NST * CH) + n * CH + c, 1)],
                                           ALU.mult, ALU.add).then_inc(s_scan, 1)

            def save(g, n):
                dve.wait_ge(s_scan, 2 * (g * NST + n) + 2)
                dve.tensor_copy(hstate[:, bass.ds((g + SEQS) * (NST * CH) + (n + 1 - RING) * CH, RING * CH)],
                                hbuf[:, :, :, HALF - 1].rearrange("p n c -> p (n c)")).then_inc(s_save, 1)

            def t_skip(t):
                dve.wait_ge(s_y, (t + 1) * NST)
                if not isinstance(t, int) or t >= 1:
                    dve.wait_ge(s_yg, t)
                for c in range(CH):
                    dve.scalar_tensor_tensor(out=yd[:, c, :], in0=xc[:, parity(t), c, :], scalar=dpw[:, c:c + 1],
                                             in1=ps_y[c][:, :], op0=ALU.mult, op1=ALU.add).then_inc(s_yd, 1)

            def t_stats(t):
                dve.wait_ge(s_om, t + 1)
                norm_stats(lambda j: m0[:, j * P:(j + 1) * P], tstat, tmv, s_tstat, s_tvar, tvare, tnmean, t)

            def front_at(f, n):
                for at, part in (("stats", lambda: f_stats(f)), ("carry_in", lambda: f_carry_in(f)),
                                 ("tap1", lambda: f_tap(f, 1)), ("tap2", lambda: f_tap(f, 2)),
                                 ("tap3", lambda: f_tap(f, 3)), ("carry_out", lambda: f_carry_out(f)),
                                 ("res", lambda: f_res(f)), ("lo", lambda: f_lo(f)), ("delta", lambda: f_delta(f))):
                    if n == AT[at]:
                        part()

            def step(g, first, last):
                for n in range(NST):
                    make_bx(g, n)
                    if n >= 1:
                        scan(g, n - 1)
                    elif not first:
                        scan(g - 1, NST - 1)
                    if n >= 1 and n % RING == 0:
                        save(g, n - 1)
                    elif n == 0 and not first:
                        save(g - 1, NST - 1)
                    if not last:
                        front_at(g + 1, n)
                    if not first:
                        if n == AT["skip"]:
                            t_skip(g - 1)
                        if n == AT["out_stats"]:
                            t_stats(g - 1)

            dve.memset(w_x[:, :, 32:64], 0.0)
            dve.memset(hstate[:, 0:SEQS * NST * CH], 0.0)
            dve.memset(half_neg[:, :], -0.5)
            dve.memset(ccarry[:, 0:SEQS, :, :], 0.0).then_inc(s_consts, 1)
            dve.wait_ge(s_consts, 1)
            dve.wait_ge(s_w, 16 * NW)
            for n in range(NST):
                front_at(0, n)
            run_steps(step, dve)
            scan(STEPS - 1, NST - 1)
            save(STEPS - 1, NST - 1)
            t_skip(STEPS - 1)
            t_stats(STEPS - 1)

        @block.gpsimd
        def _(pool):
            def f_rstd(f):
                pool.wait_ge(s_fvar, f + 1)
                pool.tensor_tensor(rstd[:, :], vare[:, :], half_neg[:, :], ALU.pow).then_inc(s_frstd, 1)
                pool.wait_ge(s_frstd, 2 * f + 1)
                pool.tensor_tensor(shift[:, :], nmean[:, :], rstd[:, :], ALU.mult).then_inc(s_frstd, 1)

            def f_u(f):
                pool.wait_ge(s_delta, f + 1)
                if not isinstance(f, int) or f >= 2:
                    pool.wait_ge(s_bx, (f - 1) * NST)
                pool.tensor_tensor(u[:, parity(f), :, :], delta[:, parity(f), :, :], xc[:, parity(f), :, :], ALU.mult)\
                    .then_inc(s_u, 1)

            def product(g, n):
                k = g * NST + n
                pool.wait_ge(s_scan, 2 * k + 2)
                pool.wait_ge(s_cs, k + 1)
                if not (isinstance(g, int) and k < RING):
                    pool.wait_ge(s_y, k - RING + 1)
                c = crep[:, n % RING, :].unsqueeze(1).broadcast_to([P, CH, HALF])
                pool.tensor_tensor(cm[:, n % RING, :, :], hbuf[:, n % RING, :, :], c, ALU.mult).then_inc(s_cm, 1)

            def t_gate(t):
                pool.wait_ge(s_yd, 2 * t + 2)
                if not isinstance(t, int) or t >= 1:
                    pool.wait_ge(s_om, t)
                pool.tensor_tensor(yg[:, :, :], yd[:, :, :], zs[:, parity(t), :, :], ALU.mult).then_inc(s_yg, 1)

            def t_rstd(t):
                pool.wait_ge(s_tvar, t + 1)
                pool.tensor_tensor(trstd[:, :], tvare[:, :], half_neg[:, :], ALU.pow).then_inc(s_trstd, 1)
                pool.wait_ge(s_trstd, 2 * t + 1)
                pool.tensor_tensor(tshift[:, :], tnmean[:, :], trstd[:, :], ALU.mult).then_inc(s_trstd, 1)

            def t_add(t):
                pool.wait_ge(s_on, t + 1)
                pool.wait_ge(s_xres, 16 * (t + 1))
                if not isinstance(t, int) or t >= 1:
                    pool.wait_ge(s_x1st, 16 * TT * t)
                pool.tensor_tensor(x1t[:, :, :], on[:, :, :], xres[:, :, :], ALU.add).then_inc(s_x1, 1)

            def step(g, first, last):
                for n in range(NST):
                    if n >= 1:
                        product(g, n - 1)
                    elif not first:
                        product(g - 1, NST - 1)
                    if not last and n == AT["root"]:
                        f_rstd(g + 1)
                    if not first and n == AT["gate"]:
                        t_gate(g - 1)
                    if not last and n == AT["u"]:
                        f_u(g + 1)
                    if not first and n == AT["out_root"]:
                        t_rstd(g - 1)
                    if not first and n == AT["add"]:
                        t_add(g - 1)

            pool.memset(ident[:, :], 0.0).then_inc(s_sel0, 1)
            pool.wait_ge(s_sel0, 1)
            pool.affine_select(out=ident[:, :], in_=ident[:, :], compare_op=ALU.not_equal, fill=1.0, base=0,
                               pattern=[[-1, P]], channel_multiplier=1).then_inc(s_ident, 1)
            pool.wait_ge(s_consts, 1)
            f_rstd(0)
            pool.memset(sel[:, :, :], 0.0).then_inc(s_sel0, 1)
            pool.wait_ge(s_sel0, 2)
            for part in range(3):
                pool.affine_select(out=sel[:, :, :], in_=sel[:, :, :], compare_op=ALU.not_equal, fill=1.0,
                                   base=-32 * part, pattern=[[-1, 2 * NST], [0, P]],
                                   channel_multiplier=1).then_inc(s_sel0, 1)
                pool.wait_ge(s_sel0, 3 + part)
            pool.sem_inc(s_sel, 1)
            f_u(0)
            run_steps(step, pool)
            product(STEPS - 1, NST - 1)
            t_gate(STEPS - 1)
            t_rstd(STEPS - 1)
            t_add(STEPS - 1)
GROUPS, GT = 16, 4
POS = 16
CAP = SEQS * LENGTH + P
ROW = 2 * D + 1
QUADS = 18
TILES = 4 * QUADS
SCALE = HD ** -0.5
MASKED = -1e30


def attention(nc, sem, carrier, banks, ident, half_neg, w, shared, x1, routed):
    ctx = ExitStack()

    def sb(name, shape, dt=F32):
        return ctx.enter_context(nc.sbuf_tensor(name, shape, dt))

    with ctx:
        ps_s, ps_t, ps_o, ps_ot = banks[0:2], banks[2], banks[3], banks[4]
        ps_p, ps_a, ps_l = banks[5], banks[6], banks[7]

        mask_l = sb("mask_l", [POS, P], BF16)
        mask_r = sb("mask_r", [POS, HEADS, P], BF16)
        before = sb("before", [P, P], BF16)
        ones = sb("ones", [P, P], BF16)
        xg = sb("xg", [P, 2, GT, D])
        xn = sb("b_xn", [P, 2, GT, D])
        stat = sb("b_stat", [P, GT, 6])
        mv = sb("b_mv", [P, GT, 2])
        vare = sb("b_vare", [P, GT])
        rstd = sb("b_rstd", [P, GT])
        nmean = sb("b_nmean", [P, GT])
        shift = sb("b_shift", [P, GT])
        xT = sb("b_xT", [P, GT * P])
        qT = sb("qT", [P, 2, GT * P])
        kz = sb("kz", [P, 2, GT, HEADS, P])
        va = sb("va", [P, 2, GT, HEADS, HD + 1])
        xb = sb("xb", [P, 2, GT, D])
        mx = sb("mx", [P, 2, HEADS])
        sub = sb("sub", [P, 2, HEADS, P])
        pr = sb("pr", [P, 2, HEADS, P])
        pT = sb("pT", [P, 2, HEADS, P])
        rs = sb("rs", [P, 2, HEADS])
        o = sb("o", [P, 2, HEADS, HD])
        oT = sb("oT", [P, 2, P])
        r1 = sb("r1", [P, GT, D])
        stat1 = sb("b_stat1", [P, GT, 6])
        mv1 = sb("b_mv1", [P, GT, 2])
        vare1 = sb("b_vare1", [P, GT])
        rstd1 = sb("b_rstd1", [P, GT])
        nmean1 = sb("b_nmean1", [P, GT])
        shift1 = sb("b_shift1", [P, GT])
        yn = sb("yn", [P, GT, D])
        yg = sb("yg1", [P, GT, D])
        pk = sb("pk", [P, 2, GT, ROW])
        yT = sb("yT", [P, GT * P])
        lmax = sb("lmax", [P, GT])
        eq = sb("eq", [P, GT, EXPERTS])
        eqr = sb("eqr", [P, GT, EXPERTS])
        rmax = sb("rmax", [P, GT])
        hot = sb("hot", [P, GT, EXPERTS])
        hot_h = sb("hot_h", [P, GT, EXPERTS], BF16)
        cum = sb("cum", [P, GT + 1, EXPERTS])
        cum_h = sb("cum_h", [P, GT, EXPERTS], BF16)
        pose = sb("pose", [P, GT, EXPERTS])
        dest = sb("dest", [P, GT])
        desti = sb("desti", [P, 2, GT], I32)
        cnt = sb("cnt", [P, EXPERTS])
        more = sb("more", [P, EXPERTS, SEQS * LENGTH // P])
        tiles = sb("tiles", [P, EXPERTS])
        tend = sb("tend", [P, EXPERTS])
        onesr = sb("onesr", [P, EXPERTS])
        full = sb("full", [P, TILES, EXPERTS])
        part = sb("part", [P, TILES, EXPERTS])
        te = sb("te", [P, TILES])
        tfirst = sb("tfirst", [P, TILES])
        trow = sb("trow", [P, TILES])
        live = sb("live", [P, TILES])
        bres = sb("bias_residual", [EXPERTS, DF + D])
        bmid = sb("bias_mid", [EXPERTS, DF + D], BF16)
        padrow = sb("padrow", [P, ROW])
        padi = sb("padi", [P, EXPERTS + 1], I32)
        padf = sb("padf", [P, EXPERTS + 1])

        names = """masks_cleared masks_made kz_cleared xg_loaded0 xg_loaded1 b_stats b_variance b_rstd b_normed b_transposed
            xT_copied q_projected k_projected q_copied k_copied v_projected v_copied xb_ready scores max_found max_subtracted
            probs_ready probs_transposed pT_copied values_summed sums_inverted o_ready o_transposed oT_copied
            attn_projected r1_ready r1_stats r1_variance r1_rstd r1_normed y_scaled y_ready pk_x1_loaded0 pk_x1_loaded1 y_transposed
            yT_copied logits_ready route_chain one_hot cum_ready ranks_counted dest_ready row_ids rows_scattered0 rows_scattered1
            counts_ready bias_chain table_chain pad_indices pad_row pad_scattered"""
        S = {n: sem("B_" + n) for n in names.split()}

        x1_g = x1.rearrange("(j w p) d -> j p w d", w=GT, p=P)

        def parity(j):
            return (j if isinstance(j, int) else j.guaranteed_mod_val) % 2

        def loads(j):
            return 8 * (j - parity(j)) + 16

        def past(j, n):
            if isinstance(j, int):
                return j >= n
            assert j.min_val >= n, "peel more groups"
            return True

        def at_most(count, limit):
            return min(count, limit) if isinstance(count, int) else count

        def run_slots(slot, engine):
            for j in range(-1, 5):
                slot(j)
            with engine.Fori(2, GROUPS // 2 - 1) as pair:
                slot(pair * 2 + 1)
                slot(pair * 2 + 2)
            for j in range(GROUPS - 1, GROUPS + 4):
                slot(j)

        def has(j):
            return not isinstance(j, int) or 0 <= j < GROUPS

        block = ctx.enter_context(nc.Block())

        @block.sync
        def _(sp):
            def load_x(j):
                if past(j, 2):
                    sp.wait_ge(S["b_normed"], j - 1)
                    sp.sem_inc(carrier, 1)
                    sp.wait_ge(S["b_stats"], 2 * (j - 1))
                    sp.sem_inc(carrier, 1)
                sp.dma_start(xg[:, parity(j), :, :], x1_g[bass.ds(j, 1)].rearrange("o p w d -> (o p) w d"))\
                  .then_inc(S[f"xg_loaded{parity(j)}"], 16)

            def load_pk(j):
                if past(j, 2):
                    sp.wait_ge(S[f"rows_scattered{parity(j)}"], 8 * GT * (j - parity(j)))
                    sp.sem_inc(carrier, 1)
                sp.dma_start(pk[:, parity(j), :, D:2 * D], x1_g[bass.ds(j, 1)].rearrange("o p w d -> (o p) w d"))\
                  .then_inc(S[f"pk_x1_loaded{parity(j)}"], 16)

            def slot(j):
                if has(j + 1):
                    load_x(j + 1)
                if has(j - 2):
                    load_pk(j - 2)

            run_slots(slot, sp)

        @block.tensor
        def _(pe):
            def b_transpose(j):
                pe.wait_ge(S["b_normed"], j + 1)
                if past(j, 1):
                    pe.wait_ge(S["v_copied"], j)
                if past(j, 4):
                    pe.wait_ge(S["yT_copied"], j - 3)
                for w_ in range(GT):
                    mm = pe.transpose(ps_a[:, w_ * P:(w_ + 1) * P], xn[:, parity(j), w_, :], ident[:, :])
                mm.then_inc(S["b_transposed"], 1)

            def project_q(j):
                pe.wait_ge(S["xT_copied"], j + 1)
                pe.matmul(ps_a[:, :], w["wqk"][:, 0:D], xT[:, :], start=True, stop=True).then_inc(S["q_projected"], 1)

            def project_k(j):
                pe.wait_ge(S["q_copied"], j + 1)
                pe.matmul(ps_a[:, :], w["wqk"][:, D:2 * D], xT[:, :], start=True, stop=True)\
                  .then_inc(S["k_projected"], 1)

            def project_v(j):
                pe.wait_ge(S["k_copied"], HEADS * (j + 1))
                for w_ in range(GT):
                    mm = pe.matmul(ps_a[:, w_ * D:(w_ + 1) * D], xT[:, w_ * P:(w_ + 1) * P], w["wqk"][:, 2 * D:3 * D],
                                   start=True, stop=True)
                mm.then_inc(S["v_projected"], 1)

            def scores(j, i):
                tile = j * GT + i
                if i == 0:
                    pe.wait_ge(S["k_copied"], HEADS * (j + 1))
                if not isinstance(j, int) or j * GT + i >= 2:
                    pe.wait_ge(S["max_subtracted"], tile - 1)
                pe.matmul(ps_s[i % 2][:, :], qT[:, parity(j), i * P:(i + 1) * P], kz[:, parity(j), i, :, :],
                          start=True, stop=False)
                pe.matmul(ps_s[i % 2][:, :], mask_l[:, :], mask_r[:, :, :], start=False, stop=True)\
                  .then_inc(S["scores"], 1)

            def turn_probs(j, i):
                tile = j * GT + i
                pe.wait_ge(S["probs_ready"], tile + 1)
                if not isinstance(j, int) or j * GT + i >= 1:
                    pe.wait_ge(S["pT_copied"], tile)
                for h in range(HEADS):
                    mm = pe.transpose(ps_t[:, h * P:(h + 1) * P], pr[:, i % 2, h, :], ident[:, :])
                mm.then_inc(S["probs_transposed"], 1)

            def sum_values(j, i):
                tile = j * GT + i
                pe.wait_ge(S["pT_copied"], tile + 1)
                if i == 0:
                    pe.wait_ge(S["v_copied"], j + 1)
                if not isinstance(j, int) or j * GT + i >= 1:
                    pe.wait_ge(S["o_ready"], tile)
                for h in range(HEADS):
                    mm = pe.matmul(ps_o[:, h * (HD + 1):(h + 1) * (HD + 1)], pT[:, i % 2, h, :],
                                   va[:, parity(j), i, h, :], start=True, stop=True)
                mm.then_inc(S["values_summed"], 1)

            def turn_o(j, i):
                tile = j * GT + i
                pe.wait_ge(S["o_ready"], tile + 1)
                if not isinstance(j, int) or j * GT + i >= 1:
                    pe.wait_ge(S["oT_copied"], tile)
                pe.transpose(ps_ot[:, 0:P], o[:, i % 2, :, :].rearrange("p h e -> p (h e)"), ident[:, :])\
                  .then_inc(S["o_transposed"], 1)

            def project_o(j, i):
                pe.wait_ge(S["oT_copied"], j * GT + i + 1)
                if i == 0 and past(j, 1):
                    pe.wait_ge(S["r1_ready"], j)
                pe.matmul(ps_p[:, i * D:(i + 1) * D], oT[:, i % 2, :], w["wo"][:, :], start=True, stop=True)\
                  .then_inc(S["attn_projected"], 1)

            def turn_y(j):
                pe.wait_ge(S["y_ready"], j + 1)
                pe.wait_ge(S["v_copied"], at_most(j + 4, GROUPS))
                for w_ in range(GT):
                    mm = pe.transpose(ps_a[:, w_ * P:(w_ + 1) * P], pk[:, parity(j), w_, 0:D], ident[:, :])
                mm.then_inc(S["y_transposed"], 1)

            def logits(j):
                pe.wait_ge(S["yT_copied"], j + 1)
                if past(j, 1):
                    pe.wait_ge(S["dest_ready"], j)
                for w_ in range(GT):
                    mm = pe.matmul(ps_l[:, w_ * EXPERTS:(w_ + 1) * EXPERTS], yT[:, w_ * P:(w_ + 1) * P], w["wg"][:, :],
                                   start=True, stop=True)
                mm.then_inc(S["logits_ready"], 1)

            def ranks(j):
                pe.wait_ge(S["cum_ready"], j + 1)
                pe.matmul(ps_l[:, 64:64 + GT * EXPERTS], before[:, :], hot_h[:, :, :], start=True, stop=False)
                pe.matmul(ps_l[:, 64:64 + GT * EXPERTS], ones[:, :], cum_h[:, :, :], start=False, stop=True)\
                  .then_inc(S["ranks_counted"], 1)

            pe.wait_ge(S["masks_made"], 4)
            def slot(j):
                if has(j):
                    scores(j, 1)
                if has(j - 1):
                    turn_probs(j - 1, 3)
                if has(j - 3):
                    turn_y(j - 3)
                if has(j - 1):
                    sum_values(j - 1, 2)
                if has(j - 3):
                    logits(j - 3)
                if has(j - 1):
                    turn_o(j - 1, 1)
                    project_o(j - 1, 0)
                if has(j):
                    scores(j, 2)
                    turn_probs(j, 0)
                if has(j - 1):
                    sum_values(j - 1, 3)
                    turn_o(j - 1, 2)
                if has(j + 1):
                    b_transpose(j + 1)
                if has(j):
                    scores(j, 3)
                if has(j + 1):
                    project_q(j + 1)
                if has(j):
                    turn_probs(j, 1)
                    sum_values(j, 0)
                if has(j - 1):
                    project_o(j - 1, 1)
                if has(j - 3):
                    ranks(j - 3)
                if has(j - 1):
                    turn_o(j - 1, 3)
                if has(j + 1):
                    project_k(j + 1)
                if has(j - 1):
                    project_o(j - 1, 2)
                if has(j):
                    turn_probs(j, 2)
                    sum_values(j, 1)
                if has(j - 1):
                    project_o(j - 1, 3)
                if has(j + 1):
                    scores(j + 1, 0)
                    project_v(j + 1)
                if has(j):
                    turn_o(j, 0)

            run_slots(slot, pe)
            pe.wait_ge(S["cum_ready"], GROUPS + 1)
            pe.wait_ge(S["dest_ready"], GROUPS)
            pe.matmul(ps_l[:, 0:EXPERTS], ones[:, :], cum_h[:, 0, :], start=True, stop=True)\
              .then_inc(S["counts_ready"], 1)

        @block.scalar
        def _(act):
            def b_norm(j):
                act.wait_ge(S["b_rstd"], 2 * j + 2)
                if past(j, 2):
                    act.wait_ge(S["b_transposed"], j - 1)
                    act.wait_ge(S["xb_ready"], j - 1)
                for t in range(GT):
                    i = act.activation(xn[:, parity(j), t, :], xg[:, parity(j), t, :], ACT.Identity,
                                       bias=shift[:, t:t + 1], scale=rstd[:, t:t + 1])
                i.then_inc(S["b_normed"], 1)

            def norm1(j):
                act.wait_ge(S["r1_rstd"], 2 * j + 2)
                if past(j, 1):
                    act.wait_ge(S["y_scaled"], j)
                for t in range(GT):
                    i = act.activation(yn[:, t, :], r1[:, t, :], ACT.Identity, bias=shift1[:, t:t + 1],
                                       scale=rstd1[:, t:t + 1])
                i.then_inc(S["r1_normed"], 1)

            def copy_xT(j):
                act.wait_ge(S["b_transposed"], j + 1)
                if past(j, 1):
                    act.wait_ge(S["v_projected"], j)
                act.activation(xT[:, :], ps_a[:, :], ACT.Copy).then_inc(S["xT_copied"], 1)

            def copy_q(j):
                act.wait_ge(S["q_projected"], j + 1)
                if past(j, 2):
                    act.wait_ge(S["scores"], GT * (j - 1))
                act.activation(qT[:, parity(j), :], ps_a[:, :], ACT.Identity, bias=w["bqk"][:, 0:1])\
                   .then_inc(S["q_copied"], 1)

            def copy_k(j):
                if isinstance(j, int) and j == 0:
                    act.wait_ge(S["kz_cleared"], 1)
                act.wait_ge(S["k_projected"], j + 1)
                for h in range(HEADS):
                    r = slice(h * HD, (h + 1) * HD)
                    act.activation(kz[r, parity(j), :, h, :], ps_a[r, :].rearrange("p (w k) -> p w k", w=GT),
                                   ACT.Identity, bias=w["bqk"][r, 1:2]).then_inc(S["k_copied"], 1)

            def exponent(j, i):
                tile = j * GT + i
                act.wait_ge(S["max_subtracted"], tile + 1)
                if not isinstance(j, int) or j * GT + i >= 2:
                    act.wait_ge(S["probs_transposed"], tile - 1)
                act.activation(pr[:, i % 2, :, :], sub[:, i % 2, :, :], ACT.Exp, scale=SCALE)\
                   .then_inc(S["probs_ready"], 1)

            def copy_pT(j, i):
                tile = j * GT + i
                act.wait_ge(S["probs_transposed"], tile + 1)
                if not isinstance(j, int) or j * GT + i >= 2:
                    act.wait_ge(S["values_summed"], tile - 1)
                act.activation(pT[:, i % 2, :, :], ps_t[:, :].rearrange("p (h q) -> p h q", h=HEADS), ACT.Copy)\
                   .then_inc(S["pT_copied"], 1)

            def copy_oT(j, i):
                tile = j * GT + i
                act.wait_ge(S["o_transposed"], tile + 1)
                if not isinstance(j, int) or j * GT + i >= 2:
                    act.wait_ge(S["attn_projected"], tile - 1)
                act.activation(oT[:, i % 2, :], ps_ot[:, 0:P], ACT.Copy).then_inc(S["oT_copied"], 1)

            def copy_yT(j):
                act.wait_ge(S["y_transposed"], j + 1)
                if past(j, 1):
                    act.wait_ge(S["logits_ready"], j)
                act.activation(yT[:, :], ps_a[:, :], ACT.Copy).then_inc(S["yT_copied"], 1)

            def slot(j):
                if has(j):
                    exponent(j, 0)
                if has(j - 1):
                    copy_pT(j - 1, 3)
                if has(j - 3):
                    copy_yT(j - 3)
                if has(j - 1):
                    copy_oT(j - 1, 1)
                if has(j + 1):
                    b_norm(j + 1)
                if has(j):
                    copy_pT(j, 0)
                    exponent(j, 1)
                if has(j + 1):
                    copy_xT(j + 1)
                if has(j - 1):
                    copy_oT(j - 1, 2)
                if has(j - 2):
                    norm1(j - 2)
                if has(j + 1):
                    copy_q(j + 1)
                if has(j):
                    exponent(j, 2)
                    copy_pT(j, 1)
                if has(j - 1):
                    copy_oT(j - 1, 3)
                if has(j + 1):
                    copy_k(j + 1)
                if has(j):
                    exponent(j, 3)
                    copy_pT(j, 2)
                    copy_oT(j, 0)

            run_slots(slot, act)

        @block.vector
        def _(dve):
            def stats(src, st, mean_var, s_bn, s_var, var_eps, less_mean, j):
                for t in range(GT):
                    i = dve.bn_stats(st[:, t, :], src(t))
                i.then_inc(s_bn, 1)
                dve.wait_ge(s_bn, 2 * j + 1)
                dve.sem_inc(carrier, 1)
                for t in range(GT):
                    i = dve.bn_aggr(mean_var[:, t, :], st[:, t, :])
                i.then_inc(s_bn, 1)
                dve.wait_ge(s_bn, 2 * j + 2)
                dve.tensor_scalar(var_eps[:, :], mean_var[:, :, 1], EPS, None, ALU.add)
                dve.tensor_scalar(less_mean[:, :], mean_var[:, :, 0], -1.0, None, ALU.mult).then_inc(s_var, 1)

            def b_stats(j):
                dve.wait_ge(S[f"xg_loaded{parity(j)}"], loads(j))
                stats(lambda t: xg[:, parity(j), t, :], stat, mv, S["b_stats"], S["b_variance"], vare, nmean, j)
                if isinstance(j, int) and j == 0:
                    dve.memset(kz[:, 0, :, :, :], 0.0)
                    dve.memset(kz[:, 1, :, :, :], 0.0).then_inc(S["kz_cleared"], 1)

            def copy_v(j):
                dve.wait_ge(S["v_projected"], j + 1)
                if past(j, 2):
                    dve.wait_ge(S["values_summed"], GT * (j - 1))
                bias = w["rows"][:, 0, :].rearrange("p (h e) -> p h e", h=HEADS).unsqueeze(1)
                dve.tensor_tensor(va[:, parity(j), :, :, 0:HD],
                                  ps_a[:, :].rearrange("p (w h e) -> p w h e", w=GT, h=HEADS),
                                  bias.broadcast_to([P, GT, HEADS, HD]), ALU.add).then_inc(S["v_copied"], 1)

            def less_max(j, i):
                tile = j * GT + i
                sc = ps_s[i % 2][:, :].rearrange("p (h k) -> p h k", h=HEADS)
                dve.wait_ge(S["scores"], tile + 1)
                dve.tensor_reduce(mx[:, i % 2, :], sc, AX.X, ALU.max).then_inc(S["max_found"], 1)
                if not isinstance(j, int) or j * GT + i >= 2:
                    dve.wait_ge(S["probs_ready"], tile - 1)
                dve.wait_ge(S["max_found"], tile + 1)
                dve.tensor_tensor(sub[:, i % 2, :, :], sc, mx[:, i % 2, :].unsqueeze(2).broadcast_to([P, HEADS, P]),
                                  ALU.subtract).then_inc(S["max_subtracted"], 1)

            def norm_o(j, i):
                tile = j * GT + i
                po = ps_o[:, 0:HEADS * (HD + 1)].rearrange("p (h e) -> p h e", h=HEADS)
                dve.wait_ge(S["values_summed"], tile + 1)
                dve.reciprocal(rs[:, i % 2, :], po[:, :, HD]).then_inc(S["sums_inverted"], 1)
                if not isinstance(j, int) or j * GT + i >= 2:
                    dve.wait_ge(S["o_transposed"], tile - 1)
                dve.wait_ge(S["sums_inverted"], tile + 1)
                dve.tensor_tensor(o[:, i % 2, :, :], po[:, :, 0:HD],
                                  rs[:, i % 2, :].unsqueeze(2).broadcast_to([P, HEADS, HD]), ALU.mult)\
                   .then_inc(S["o_ready"], 1)

            def residual(j):
                dve.wait_ge(S["attn_projected"], GT * (j + 1))
                dve.wait_ge(S["xb_ready"], j + 1)
                if past(j, 1):
                    dve.wait_ge(S["r1_normed"], j)
                dve.tensor_tensor(r1[:, :, :], ps_p[:, :].rearrange("p (w d) -> p w d", w=GT), xb[:, parity(j), :, :],
                                  ALU.add).then_inc(S["r1_ready"], 1)
                dve.wait_ge(S["r1_ready"], j + 1)
                stats(lambda t: r1[:, t, :], stat1, mv1, S["r1_stats"], S["r1_variance"], vare1, nmean1, j)

            def choose(j):
                lg = ps_l[:, 0:GT * EXPERTS].rearrange("p (w e) -> p w e", w=GT)
                chain, c = S["route_chain"], 5
                dve.wait_ge(S["logits_ready"], j + 1)
                if past(j, 1):
                    dve.wait_ge(S["dest_ready"], j)
                dve.tensor_reduce(lmax[:, :], lg, AX.X, ALU.max).then_inc(chain, 1)
                dve.wait_ge(chain, c * j + 1)
                dve.tensor_tensor(eq[:, :, :], lg, lmax[:, :].unsqueeze(2).broadcast_to([P, GT, EXPERTS]), ALU.is_equal)\
                   .then_inc(chain, 1)
                dve.wait_ge(chain, c * j + 2)
                order = shared["order"][:, :].unsqueeze(1).broadcast_to([P, GT, EXPERTS])
                dve.tensor_tensor(eqr[:, :, :], eq[:, :, :], order, ALU.mult).then_inc(chain, 1)
                dve.wait_ge(chain, c * j + 3)
                dve.tensor_reduce(rmax[:, :], eqr[:, :, :], AX.X, ALU.max).then_inc(chain, 1)
                dve.wait_ge(chain, c * j + 4)
                dve.tensor_tensor(hot[:, :, :], eqr[:, :, :], rmax[:, :].unsqueeze(2).broadcast_to([P, GT, EXPERTS]),
                                  ALU.is_equal).then_inc(chain, 1)
                dve.wait_ge(chain, c * j + 5)
                if past(j, 1):
                    dve.wait_ge(S["ranks_counted"], j)
                dve.tensor_copy(hot_h[:, :, :], hot[:, :, :])
                for t in range(GT):
                    dve.tensor_tensor(cum[:, t + 1, :], cum[:, t, :], hot[:, t, :], ALU.add)\
                       .then_inc(S["one_hot"], 1)
                    dve.wait_ge(S["one_hot"], (GT + 2) * j + t + 1)
                dve.tensor_copy(cum_h[:, :, :], cum[:, 0:GT, :]).then_inc(S["one_hot"], 1)
                dve.wait_ge(S["one_hot"], (GT + 2) * j + GT + 1)
                dve.tensor_copy(cum[:, 0, :], cum[:, GT, :]).then_inc(S["one_hot"], 1)
                dve.wait_ge(S["one_hot"], (GT + 2) * j + GT + 2)
                dve.sem_inc(S["cum_ready"], 1)

            def place(j):
                if past(j, 1):
                    dve.wait_ge(S["dest_ready"], j)
                dve.wait_ge(S["ranks_counted"], j + 1)
                dve.tensor_tensor(pose[:, :, :], ps_l[:, 64:64 + GT * EXPERTS].rearrange("p (w e) -> p w e", w=GT),
                                  shared["region"][:, :].unsqueeze(1).broadcast_to([P, GT, EXPERTS]), ALU.add)\
                   .then_inc(S["row_ids"], 1)
                dve.wait_ge(S["row_ids"], 5 * j + 1)
                dve.tensor_tensor(pose[:, :, :], pose[:, :, :], hot[:, :, :], ALU.mult).then_inc(S["row_ids"], 1)
                dve.wait_ge(S["row_ids"], 5 * j + 2)
                dve.tensor_reduce(dest[:, :], pose[:, :, :], AX.X, ALU.add).then_inc(S["row_ids"], 1)
                dve.wait_ge(S["row_ids"], 5 * j + 3)
                if past(j, 2):
                    dve.wait_ge(S[f"rows_scattered{parity(j)}"], 8 * GT * (j - parity(j)))
                dve.tensor_copy(desti[:, parity(j), :], dest[:, :]).then_inc(S["row_ids"], 1)
                dve.tensor_copy(pk[:, parity(j), :, 2 * D].bitcast(I32), shared["ids"][:, bass.ds(j * GT, GT)])\
                   .then_inc(S["row_ids"], 1)
                dve.wait_ge(S["row_ids"], 5 * j + 5)
                dve.sem_inc(S["dest_ready"], 1)

            dve.memset(w["bias_parts"][:, :], 0.0)
            dve.memset(cum[:, 0, :], 0.0)
            dve.memset(va[:, :, :, :, HD:HD + 1], 1.0).then_inc(S["bias_chain"], 1)
            dve.wait_ge(S["bias_chain"], 1)
            def slot(j):
                if has(j - 1):
                    norm_o(j - 1, 1)
                if has(j):
                    less_max(j, 0)
                    copy_v(j)
                if has(j + 1):
                    b_stats(j + 1)
                if has(j - 2):
                    residual(j - 2)
                if has(j - 1):
                    norm_o(j - 1, 2)
                if has(j):
                    less_max(j, 1)
                if has(j - 3):
                    choose(j - 3)
                if has(j - 1):
                    norm_o(j - 1, 3)
                if has(j):
                    less_max(j, 2)
                    norm_o(j, 0)
                    less_max(j, 3)
                if has(j - 3):
                    place(j - 3)

            run_slots(slot, dve)

            chain = S["table_chain"]
            steps = [0]

            def link(i):
                steps[0] += 1
                i.then_inc(chain, 1)
                dve.wait_ge(chain, steps[0])

            dve.wait_ge(S["one_hot"], (GT + 2) * GROUPS)
            dve.wait_ge(S["ranks_counted"], GROUPS)
            dve.tensor_copy(cum_h[:, 0, :], cum[:, 0, :]).then_inc(S["cum_ready"], 1)
            link(dve.memset(onesr[:, :], 1.0))
            dve.wait_ge(S["counts_ready"], 1)
            link(dve.tensor_copy(cnt[:, :], ps_l[:, 0:EXPERTS]))
            link(dve.tensor_tensor(padf[:, 0:EXPERTS], cnt[:, :], shared["pad"][:, 0:EXPERTS], ALU.add))
            link(dve.tensor_copy(padf[:, EXPERTS:], shared["pad"][:, EXPERTS:EXPERTS + 1]))
            dve.tensor_copy(padi[:, :], padf[:, :]).then_inc(S["pad_indices"], 1)
            n128 = SEQS * LENGTH // P
            link(dve.tensor_tensor(more[:, :, :], cnt[:, :].unsqueeze(2).broadcast_to([P, EXPERTS, n128]),
                                   shared["multiples"][:, :].unsqueeze(1).broadcast_to([P, EXPERTS, n128]), ALU.is_gt))
            link(dve.tensor_reduce(tiles[:, :], more[:, :, :], AX.X, ALU.add))
            link(dve.tensor_tensor_scan(tend[:, :], onesr[:, :], tiles[:, :], 0.0, ALU.mult, ALU.add))
            index = shared["index"][:, :].unsqueeze(2).broadcast_to([P, TILES, EXPERTS])
            link(dve.tensor_tensor(full[:, :, :], tend[:, :].unsqueeze(1).broadcast_to([P, TILES, EXPERTS]), index,
                                   ALU.is_le))
            link(dve.tensor_reduce(te[:, :], full[:, :, :], AX.X, ALU.add))
            link(dve.tensor_tensor(part[:, :, :], full[:, :, :],
                                   tiles[:, :].unsqueeze(1).broadcast_to([P, TILES, EXPERTS]), ALU.mult))
            link(dve.tensor_reduce(tfirst[:, :], part[:, :, :], AX.X, ALU.add))
            link(dve.tensor_tensor(trow[:, :], shared["index"][:, :], tfirst[:, :], ALU.subtract))
            link(dve.tensor_scalar(live[:, :], te[:, :], float(EXPERTS), float(P), ALU.is_lt, ALU.mult))
            link(dve.tensor_tensor(trow[:, :], trow[:, :], live[:, :], ALU.mult))
            link(dve.scalar_tensor_tensor(out=trow[:, :], in0=te[:, :], scalar=float(CAP), in1=trow[:, :],
                                          op0=ALU.mult, op1=ALU.add))
            link(dve.tensor_copy(shared["tile_row"][:, :], trow[0:1, :]))
            link(dve.tensor_scalar(te[:, :], te[:, :], float(EXPERTS - 1), None, ALU.min))
            link(dve.tensor_copy(shared["tile_expert"][:, :], te[0:1, :]))

            bf, bparts, chain = w["biases"], w["bias_parts"], S["bias_chain"]
            dve.tensor_copy(bparts[0:EXPERTS, :], bf[:, :]).then_inc(chain, 1)
            dve.wait_ge(chain, 2)
            dve.tensor_tensor(bres[:, :], bf[:, :], bparts[0:EXPERTS, :], ALU.subtract).then_inc(chain, 1)
            dve.wait_ge(chain, 3)
            dve.tensor_copy(bmid[:, :], bres[:, :]).then_inc(chain, 1)
            dve.tensor_copy(bparts[32:32 + EXPERTS, :], bres[:, :]).then_inc(chain, 1)
            dve.wait_ge(chain, 5)
            dve.tensor_tensor(bparts[64:64 + EXPERTS, :], bres[:, :], bmid[:, :], ALU.subtract).then_inc(chain, 1)
            dve.wait_ge(chain, 6)

        @block.gpsimd
        def _(pool):
            pool.memset(mask_l[:, :], 0.0).then_inc(S["masks_cleared"], 1)
            pool.memset(mask_r[:, :, :], MASKED).then_inc(S["masks_cleared"], 1)
            pool.memset(before[:, :], 1.0).then_inc(S["masks_cleared"], 1)
            pool.memset(ones[:, :], 1.0).then_inc(S["masks_made"], 1)
            pool.wait_ge(S["masks_cleared"], 3)
            v = mask_l[:, :].rearrange("p (a l) -> p a l", l=POS)
            pool.affine_select(out=v, in_=v, compare_op=ALU.not_equal, fill=1.0, base=0,
                               pattern=[[0, P // POS], [-1, POS]], channel_multiplier=1).then_inc(S["masks_made"], 1)
            v = mask_r[:, :, :].rearrange("p h (a l) -> p (h a) l", l=POS)
            pool.affine_select(out=v, in_=v, compare_op=ALU.not_equal, fill=0.0, base=0,
                               pattern=[[0, HEADS * P // POS], [-1, POS]], channel_multiplier=1)\
                .then_inc(S["masks_made"], 1)
            pool.affine_select(out=before[:, :], in_=before[:, :], compare_op=ALU.is_gt, fill=0.0, base=0,
                               pattern=[[1, P]], channel_multiplier=-1).then_inc(S["masks_made"], 1)
            pool.memset(padrow[:, 0:2 * D], 0.0).then_inc(S["pad_row"], 1)
            pool.tensor_copy(padrow[:, 2 * D:].bitcast(I32), shared["ids"][:, GT * GROUPS:]).then_inc(S["pad_row"], 1)

            def root(out, var_eps, less_mean, shifted, s_var, s_out, j):
                pool.wait_ge(s_var, j + 1)
                pool.tensor_tensor(out[:, :], var_eps[:, :], half_neg[:, :], ALU.pow).then_inc(s_out, 1)
                pool.wait_ge(s_out, 2 * j + 1)
                pool.tensor_tensor(shifted[:, :], less_mean[:, :], out[:, :], ALU.mult).then_inc(s_out, 1)

            def row(i):
                return w["rows"][:, i, :].unsqueeze(1).broadcast_to([P, GT, D])

            def with_bias(j):
                pool.wait_ge(S["b_normed"], j + 1)
                if past(j, 2):
                    pool.wait_ge(S["r1_ready"], j - 1)
                pool.tensor_tensor(xb[:, parity(j), :, :], xn[:, parity(j), :, :], row(1), ALU.add)\
                    .then_inc(S["xb_ready"], 1)

            def scale_y(j):
                pool.wait_ge(S["r1_normed"], j + 1)
                if past(j, 1):
                    pool.wait_ge(S["y_ready"], j)
                pool.tensor_tensor(yg[:, :, :], yn[:, :, :], row(2), ALU.mult).then_inc(S["y_scaled"], 1)
                pool.wait_ge(S["y_scaled"], j + 1)
                if past(j, 2):
                    pool.wait_ge(S[f"rows_scattered{parity(j)}"], 8 * GT * (j - parity(j)))
                pool.tensor_tensor(pk[:, parity(j), :, 0:D], yg[:, :, :], row(3), ALU.add).then_inc(S["y_ready"], 1)

            def scatter(j):
                pool.wait_ge(S["dest_ready"], j + 1)
                pool.wait_ge(S[f"pk_x1_loaded{parity(j)}"], loads(j))
                pool.wait_ge(S["y_ready"], j + 1)
                pool.sem_inc(carrier, 1)
                for t in range(GT):
                    pool.indirect_dma_start(
                        out=routed[:, :], out_offset=bass.IndirectOffsetOnAxis(ap=desti[:, parity(j), t:t + 1], axis=0),
                        in_=pk[:, parity(j), t, :], in_offset=None).then_inc(S[f"rows_scattered{parity(j)}"], 16)

            def b_root(j):
                root(rstd, vare, nmean, shift, S["b_variance"], S["b_rstd"], j)

            def r1_root(j):
                root(rstd1, vare1, nmean1, shift1, S["r1_variance"], S["r1_rstd"], j)

            def slot(j):
                if has(j + 1):
                    b_root(j + 1)
                if has(j - 2):
                    r1_root(j - 2)
                if has(j - 4):
                    scatter(j - 4)
                if has(j):
                    with_bias(j)
                if has(j - 2):
                    scale_y(j - 2)

            run_slots(slot, pool)
            pool.wait_ge(S["pad_indices"], 1)
            pool.wait_ge(S["pad_row"], 2)
            for e in range(EXPERTS + 1):
                pool.indirect_dma_start(
                    out=routed[:, :], out_offset=bass.IndirectOffsetOnAxis(ap=padi[:, e:e + 1], axis=0),
                    in_=padrow[:, :], in_offset=None).then_inc(S["pad_scattered"], 16)
            pool.wait_ge(S["pad_scattered"], 16 * (EXPERTS + 1))
            for i in range(2):
                pool.wait_ge(S[f"rows_scattered{i}"], 8 * GT * GROUPS)


def experts(nc, sem, banks, sel, ident, half_neg, w, shared, carrier, routed, out):
    ctx = ExitStack()
    SLOTS = 4

    def sb(name, shape, dt=F32):
        return ctx.enter_context(nc.sbuf_tensor(name, shape, dt))

    with ctx:
        ps_yt, ps_h, ps_f = banks[0:2], banks[2:4], banks[4:6]

        rows = sb("rows", [P, SLOTS, 4, ROW])
        yT = sb("d_yT", [P, 2, P])
        w1 = sb("w1_of_tile", [P, 2, DF])
        hT = sb("hT", [P, 2, DF // P, P])
        bparts = w["bias_parts"]
        z0 = sb("z0", [P, 4, D])
        z1 = sb("z1", [P, 4, D])
        z2 = sb("z2", [P, 4, D])
        z3 = sb("z3", [P, 4, D])
        z4 = sb("z4", [P, 4, D])
        res = sb("res", [P, 2, 4, D])
        tokens = sb("tokens", [P, 2, 4], I32)
        stat = [sb(f"d_stat{i}", [P, 4, 6]) for i in range(2)]
        mv = [sb(f"d_mv{i}", [P, 4, 2]) for i in range(2)]
        vare = [sb(f"d_vare{i}", [P, 4]) for i in range(2)]
        rstd = [sb(f"d_rstd{i}", [P, 4]) for i in range(2)]

        names = """rows_loaded0 rows_loaded1 rows_loaded2 rows_loaded3 y_transposed yT_copied hidden_summed
            w1_copied hidden_ready expert_summed z0_ready stats0 stats1 variance0 variance1
            rstd0 rstd1 z1_ready z2_ready z3_ready z4_ready res_ready
            out_scattered0 out_scattered1"""
        S = {n: sem("D_" + n) for n in names.split()}

        def fixed(q, n):
            if isinstance(q, int):
                return q % n
            assert q.out_of_modulus % n == 0
            return q.guaranteed_mod_val % n

        def past(q, n):
            if isinstance(q, int):
                return q >= n
            assert q.min_val >= n, "peel more quads"
            return True

        def run_slots(slot, engine):
            for q in range(SLOTS):
                slot(q)
            with engine.Fori(1, QUADS // SLOTS) as turn:
                for i in range(SLOTS):
                    slot(turn * SLOTS + i)
            for q in range(QUADS // SLOTS * SLOTS, QUADS + 2):
                slot(q)

        def lagged(q, i, lag):
            q, i = (q, i - lag) if i >= lag else (q - 1, i - lag + 4)
            if isinstance(q, int) and not 0 <= q < QUADS:
                return None
            return q, i

        block = ctx.enter_context(nc.Block())

        @block.sync
        def _(sp):
            def load(q):
                if past(q, SLOTS):
                    sp.wait_ge(S["res_ready"], 2 * (q - SLOTS + 1))
                    sp.sem_inc(carrier, 1)
                for i in range(4):
                    first = sp.value_load(shared["tile_row"][0:1, bass.ds(q * 4 + i, 1)], min_val=0,
                                          max_val=EXPERTS * CAP)
                    sp.dma_start(rows[:, fixed(q, SLOTS), i, :], routed[bass.ds(first, P), :])\
                      .then_inc(S[f"rows_loaded{fixed(q, SLOTS)}"], 16)

            def slot(q):
                if not isinstance(q, int) or q + 1 < QUADS:
                    load(q + 1)

            load(0)
            run_slots(slot, sp)
            for s in range(2):
                sp.wait_ge(S[f"out_scattered{s}"], 32 * QUADS)

        @block.tensor
        def _(pe):
            def turn_y(q, i):
                tile = q * 4 + i
                if i == 0:
                    s = fixed(q, SLOTS)
                    pe.wait_ge(S[f"rows_loaded{s}"], (q - s) // SLOTS * 64 + 64)
                if not isinstance(q, int) or tile >= 2:
                    pe.wait_ge(S["yT_copied"], tile - 1)
                pe.transpose(ps_yt[i % 2][:, 0:P], rows[:, fixed(q, SLOTS), i, 0:D], ident[:, :])\
                  .then_inc(S["y_transposed"], 1)

            def expert_of(tile):
                return pe.value_load(shared["tile_expert"][0:1, bass.ds(tile, 1)], min_val=0, max_val=EXPERTS - 1)

            def hidden(q, i):
                tile = q * 4 + i
                e = expert_of(tile)
                if not isinstance(q, int) or tile >= 2:
                    pe.wait_ge(S["hidden_ready"], tile - 1)
                pe.wait_ge(S["yT_copied"], tile + 1)
                pe.wait_ge(S["w1_copied"], tile + 1)
                one = sel[:, bass.ds(e, 1), :].rearrange("p o m -> p (o m)")
                for k in range(DF // P):
                    dst = ps_h[i % 2][:, k * P:(k + 1) * P]
                    pe.matmul(dst, bparts[:, k * P:(k + 1) * P], one, start=True, stop=False)
                    mm = pe.matmul(dst, w1[:, i % 2, k * P:(k + 1) * P], yT[:, i % 2, :], start=False, stop=True)
                mm.then_inc(S["hidden_summed"], 1)

            def outward(q, i):
                tile = q * 4 + i
                e = expert_of(tile)
                if i == 0 and past(q, 2):
                    pe.wait_ge(S["z0_ready"], q - 1)
                dst = ps_f[fixed(q, 2)][:, i * D:(i + 1) * D]
                pe.matmul(dst, sel[:, bass.ds(e, 1), :].rearrange("p o m -> p (o m)"), bparts[:, DF:], start=True,
                          stop=False)
                pe.wait_ge(S["hidden_ready"], tile + 1)
                for k in range(DF // P):
                    mm = pe.matmul(dst, hT[:, i % 2, k, :],
                                   w["w2"][:, bass.ds(e, 1), k, :].rearrange("p o d -> p (o d)"),
                                   start=False, stop=k == DF // P - 1)
                mm.then_inc(S["expert_summed"], 1)

            def slot(q):
                for i in range(4):
                    for lag, part in enumerate((turn_y, hidden, outward)):
                        at = lagged(q, i, lag)
                        if at:
                            part(*at)

            run_slots(slot, pe)

        @block.scalar
        def _(act):
            def copy_yT(q, i):
                tile = q * 4 + i
                act.wait_ge(S["y_transposed"], tile + 1)
                if not isinstance(q, int) or tile >= 2:
                    act.wait_ge(S["hidden_summed"], tile - 1)
                act.activation(yT[:, i % 2, :], ps_yt[i % 2][:, 0:P], ACT.Copy).then_inc(S["yT_copied"], 1)

            def copy_w1(q, i):
                tile = q * 4 + i
                e = act.value_load(shared["tile_expert"][0:1, bass.ds(tile, 1)], min_val=0, max_val=EXPERTS - 1)
                if not isinstance(q, int) or tile >= 2:
                    act.wait_ge(S["hidden_summed"], tile - 1)
                    act.sem_inc(carrier, 1)
                act.activation(w1[:, i % 2, :], w["w1"][:, bass.ds(e, 1), :].rearrange("p o f -> p (o f)"), ACT.Copy)\
                   .then_inc(S["w1_copied"], 1)

            def relu(q, i):
                tile = q * 4 + i
                act.wait_ge(S["hidden_summed"], tile + 1)
                if not isinstance(q, int) or tile >= 2:
                    act.wait_ge(S["expert_summed"], tile - 1)
                act.activation(hT[:, i % 2, :, :], ps_h[i % 2][:, :].rearrange("p (k t) -> p k t", t=P), ACT.Relu)\
                   .then_inc(S["hidden_ready"], 1)

            def slot(q):
                for i in range(4):
                    for lag, part in ((0, copy_yT), (0, copy_w1), (1, relu)):
                        at = lagged(q, i, lag)
                        if at:
                            part(*at)

            run_slots(slot, act)

        @block.vector
        def _(dve):
            def stats(src, n, q):
                s_bn = S[f"stats{n}"]
                for t in range(4):
                    i = dve.bn_stats(stat[n][:, t, :], src[:, t, :])
                i.then_inc(s_bn, 1)
                dve.wait_ge(s_bn, 2 * q + 1)
                dve.sem_inc(carrier, 1)
                for t in range(4):
                    i = dve.bn_aggr(mv[n][:, t, :], stat[n][:, t, :])
                i.then_inc(s_bn, 1)
                dve.wait_ge(s_bn, 2 * q + 2)
                dve.tensor_scalar(vare[n][:, :], mv[n][:, :, 1], EPS, None, ALU.add).then_inc(S[f"variance{n}"], 1)

            def norm(dst, src, n, q, done):
                dve.wait_ge(S[f"rstd{n}"], q + 1)
                for t in range(4):
                    i = dve.tensor_scalar(dst[:, t, :], src[:, t, :], mv[n][:, t, 0:1], rstd[n][:, t:t + 1],
                                          ALU.subtract, ALU.mult)
                i.then_inc(S[done], 1)

            def add_y(q):
                dve.wait_ge(S["expert_summed"], 4 * (q + 1))
                if past(q, 1):
                    dve.wait_ge(S["z1_ready"], q)
                dve.tensor_tensor(z0[:, :, :], ps_f[fixed(q, 2)][:, :].rearrange("p (t d) -> p t d", t=4),
                                  rows[:, fixed(q, SLOTS), :, 0:D], ALU.add).then_inc(S["z0_ready"], 1)
                dve.wait_ge(S["z0_ready"], q + 1)
                stats(z0, 0, q)

            def norm2(q):
                if past(q, 1):
                    dve.wait_ge(S["z2_ready"], q)
                norm(z1, z0, 0, q, "z1_ready")

            def row(i):
                return w["rows"][:, i, :].unsqueeze(1).broadcast_to([P, 4, D])

            def affine(q):
                dve.wait_ge(S["z1_ready"], q + 1)
                if past(q, 1):
                    dve.wait_ge(S["z3_ready"], q)
                dve.tensor_tensor(z2[:, :, :], z1[:, :, :], row(4), ALU.mult).then_inc(S["z2_ready"], 1)
                dve.wait_ge(S["z2_ready"], q + 1)
                if past(q, 1):
                    dve.wait_ge(S["z4_ready"], q)
                dve.tensor_tensor(z3[:, :, :], z2[:, :, :], row(5), ALU.add).then_inc(S["z3_ready"], 1)

            def stats2(q):
                dve.wait_ge(S["z3_ready"], q + 1)
                stats(z3, 1, q)

            def norm3(q):
                if past(q, 1):
                    dve.wait_ge(S["res_ready"], 2 * q)
                norm(z4, z3, 1, q, "z4_ready")

            def quad(q):
                return not isinstance(q, int) or 0 <= q < QUADS

            def slot(q):
                for i in range(4):
                    if i == 2 and quad(q - 1):
                        add_y(q - 1)
                    if i == 2 and quad(q - 2):
                        norm3(q - 2)
                    if i == 3 and quad(q - 1):
                        norm2(q - 1)
                        affine(q - 1)
                        stats2(q - 1)

            run_slots(slot, dve)

        @block.gpsimd
        def _(pool):
            def root(n, q):
                pool.wait_ge(S[f"variance{n}"], q + 1)
                pool.tensor_tensor(rstd[n][:, :], vare[n][:, :], half_neg[:, :], ALU.pow).then_inc(S[f"rstd{n}"], 1)

            def add_x1(q):
                par = fixed(q, SLOTS)
                pool.wait_ge(S["z4_ready"], q + 1)
                if past(q, 2):
                    s = fixed(q, 2)
                    pool.wait_ge(S[f"out_scattered{s}"], 32 * (q - s))
                pool.tensor_tensor(res[:, fixed(q, 2), :, :], z4[:, :, :], rows[:, par, :, D:2 * D], ALU.add)\
                    .then_inc(S["res_ready"], 1)
                pool.tensor_copy(tokens[:, fixed(q, 2), :], rows[:, par, :, 2 * D].bitcast(I32))\
                    .then_inc(S["res_ready"], 1)

            def scatter(q):
                pool.wait_ge(S["res_ready"], 2 * q + 2)
                pool.sem_inc(carrier, 1)
                for i in range(4):
                    pool.indirect_dma_start(
                        out=out[:, :],
                        out_offset=bass.IndirectOffsetOnAxis(ap=tokens[:, fixed(q, 2), i:i + 1], axis=0),
                        in_=res[:, fixed(q, 2), i, :], in_offset=None, bounds_check=SEQS * LENGTH - 1,
                        oob_is_err=False).then_inc(S[f"out_scattered{fixed(q, 2)}"], 16)

            def quad(q):
                return not isinstance(q, int) or 0 <= q < QUADS

            def slot(q):
                if quad(q - 2):
                    root(1, q - 2)
                if quad(q - 1):
                    root(0, q - 1)
                if quad(q - 2):
                    add_x1(q - 2)
                    scatter(q - 2)

            run_slots(slot, pool)


def build(nc, x, w_in_t, per_channel, w_x_t, w_dt_t, w_out_t, wqkv_t, bqk, wo_t, wg_t, rows, biases, w1, w2,
          consts, ids, out):
    x1 = nc.dram_tensor("x1_rows", [SEQS * LENGTH, D], F32, kind="Internal").ap()
    routed = nc.dram_tensor("routed", [EXPERTS * CAP + P, ROW], F32, kind="Internal").ap()
    with ExitStack() as ctx:
        def sb(name, shape, dt=F32):
            return ctx.enter_context(nc.sbuf_tensor(name, shape, dt))

        def sem(name):
            return ctx.enter_context(nc.semaphore(name))

        banks = [ctx.enter_context(nc.psum_tensor(f"bank{i}", [P, 512], F32)) for i in range(8)]
        sel = sb("sel", [96, 2 * NST, P], BF16)
        ident = sb("ident", [P, P])
        half_neg = sb("half_neg", [P, 4])
        w = {"wqk": sb("w_qkv", [P, 3 * D]), "bqk": sb("b_qk", [P, 2]), "wo": sb("w_o", [P, D]),
             "wg": sb("w_g", [P, EXPERTS]), "rows": sb("row_params", [P, 6, D]),
             "w1": sb("w_1", [P, EXPERTS, DF]), "w2": sb("w_2", [P, EXPERTS, DF // P, D]),
             "biases": sb("biases", [EXPERTS, DF + D]), "bias_parts": sb("bias_parts", [96, DF + D], BF16)}
        table = sb("table", [P, consts.shape[1]])
        idt = sb("idt", [P, ids.shape[1]], I32)
        at, shared = 0, {"ids": idt, "tile_row": sb("tile_row", [1, TILES], I32),
                         "tile_expert": sb("tile_expert", [1, TILES], I32)}
        for name, n in TABLE:
            shared[name] = table[:, at:at + n]
            at += n
        late = [(w["wqk"][:, :], wqkv_t), (w["bqk"][:, :], bqk), (w["wo"][:, :], wo_t), (w["wg"][:, :], wg_t),
                (w["rows"][:, :, :].rearrange("p i d -> p (i d)"), rows.partition_broadcast(P)),
                (table[:, :], consts), (idt[:, :], ids), (w["biases"][:, :], biases),
                (w["w1"][:, :, :], w1.rearrange("e p f -> p e f")),
                (w["w2"][:, :, :, :], w2.rearrange("e (k p) d -> p e k d", p=P))]
        carrier = sem("waits_carried")
        s_late = sem("late_weights_loaded")
        mamba(nc, sem, carrier, banks, sel, ident, half_neg, x, w_in_t, per_channel, w_x_t, w_dt_t, w_out_t, x1,
              late, s_late)
        attention(nc, sem, carrier, banks, ident, half_neg, w, shared, x1, routed)
        experts(nc, sem, banks, sel, ident, half_neg, w, shared, carrier, routed, out)


TABLE = (("order", EXPERTS), ("region", EXPERTS), ("pad", EXPERTS + 1), ("multiples", SEQS * LENGTH // P),
         ("index", TILES))


def kernel(**inputs):
    import numpy as np
    import concourse.bacc as bacc
    from concourse.bass_utils import run_bass_kernel_spmd

    a = {k: np.asarray(v) for k, v in inputs.items()}

    def lay(v):
        return np.ascontiguousarray(v)

    def blocks(name):
        return a[name].reshape(CH, P, -1).transpose(1, 0, 2).reshape(P, -1)

    p = np.arange(P)
    cols = {"order": np.tile(EXPERTS - np.arange(EXPERTS), (P, 1)),
            "region": np.tile(CAP * np.arange(EXPERTS), (P, 1)),
            "pad": p[:, None] + CAP * np.arange(EXPERTS + 1)[None, :],
            "multiples": np.tile(P * np.arange(SEQS * LENGTH // P), (P, 1)),
            "index": np.tile(np.arange(TILES), (P, 1))}
    consts = np.concatenate([cols[name] for name, _ in TABLE], 1).astype(np.float32)
    tile, half = np.divmod(np.arange(GROUPS * GT), 2)
    ids = (p[:, None] // POS) * LENGTH + p[:, None] % POS + half[None, :] * HALF + tile[None, :] * POS
    ids = np.concatenate([ids, np.full((P, 1), 1 << 20)], 1).astype(np.int32)

    arrays = {
        "x": a["L0_attn_x"].reshape(SEQS, 2, HALF, D).transpose(1, 0, 2, 3).reshape(-1, D),
        "w_in_t": a["L0_attn_W_in"].T,
        "per_channel": np.concatenate([blocks("L0_attn_" + n) for n in ("conv_w", "conv_b", "b_dt", "Dp", "A_log")], 1),
        "w_x_t": a["L0_attn_W_x"].T,
        "w_dt_t": a["L0_attn_W_dt"].T,
        "w_out_t": a["L0_attn_W_out"].T,
        "wqkv_t": a["L0_ffn_Wqkv"].T,
        "bqk": a["L0_ffn_bqkv"][0:2 * D].reshape(2, D).T,
        "wo_t": a["L0_ffn_Wo"].T,
        "wg_t": a["L0_ffn_Wg"].T,
        "rows": np.concatenate([a["L0_ffn_bqkv"][2 * D:]] + [a["L0_ffn_" + n] for n in ("bo", "g1", "be1", "g2", "be2")]),
        "biases": np.concatenate([a["L0_ffn_b1"], a["L0_ffn_b2"]], 1),
        "w1": a["L0_ffn_W1"],
        "w2": a["L0_ffn_W2"],
        "consts": consts,
        "ids": ids,
    }
    nc = bacc.Bacc("TRN2", target_bir_lowering=False, num_devices=1)
    arrays = {"in_" + k: lay(v) for k, v in arrays.items()}
    args = [nc.dram_tensor(k, v.shape, mybir.dt.from_np(v.dtype), kind="ExternalInput").ap() for k, v in arrays.items()]
    out = nc.dram_tensor("out", [SEQS * LENGTH, D], F32, kind="ExternalOutput").ap()
    build(nc, *args, out)
    r = run_bass_kernel_spmd(nc, [arrays], core_ids=[0])
    return r.results[0]["out"].reshape(SEQS, LENGTH, D)
```
